# Optimizing a Trainium2 kernel written in Bass

```python
import numpy as np
import jax
import jax.numpy as jnp

def _softmax(x, axis=-1):
    return jax.nn.softmax(x, axis=axis)

def _gelu(x):
    return jax.nn.gelu(x, approximate=True)

def _silu(x):
    return jax.nn.silu(x)

def _sigmoid(x):
    return jax.nn.sigmoid(x)

def _layernorm(x, axis=-1, eps=1e-05):
    m = jnp.mean(x, axis=axis, keepdims=True)
    v = jnp.var(x, axis=axis, keepdims=True)
    return (x - m) / jnp.sqrt(v + eps)

def _scatter_add(tgt, idx, src, axis=0):
    return tgt.at[idx].add(src)

def _segment_sum(src, seg, n):
    return jax.ops.segment_sum(src, seg, n)
kernel_name = 'mk_decoder_postln_d1_seqx_r8_4365b9'

def setup_inputs(seed: int=0):
    np.random.seed(seed)
    _w = jnp.asarray

    def _rec_inputs():
        import jax
        import jax.numpy as jnp
        _rk = jax.random.key(seed)
        x = -0.0003929 + 0.9999 * jax.random.normal(jax.random.fold_in(_rk, 1), (8, 128, 128), jnp.float32)
        _lenS = 128 - jax.random.randint(jax.random.fold_in(_rk, 7), (8,), 0, max(1, 128 // 4) + 1, jnp.int32)
        _lenS2 = 77 - jax.random.randint(jax.random.fold_in(_rk, 8), (8,), 0, max(1, 77 // 4) + 1, jnp.int32)
        _ctx_1024P = jax.random.normal(jax.random.fold_in(_rk, 11), (8, 16, 128), jnp.float32)
        _ctx_1024c = jax.random.dirichlet(jax.random.fold_in(_rk, 511), 0.3 * jnp.ones((16,), jnp.float32), (8, 77))
        _ctx_1024t = jnp.einsum('bsk,bkd->bsd', _ctx_1024c, _ctx_1024P)
        _ctx_1024t = _ctx_1024t * jax.lax.rsqrt(jnp.mean(jnp.square(_ctx_1024t)) + 1e-12) * 0.953939
        ctx_1024 = -3.05549e-07 + 0.0199987 * (_ctx_1024t + 0.3 * jax.random.normal(jax.random.fold_in(_rk, 611), (8, 77, 128), jnp.float32))
        return (x, ctx_1024)
    x, ctx_1024 = _rec_inputs()

    def _L0_attn_setup():
        import jax, jax.numpy as jnp
        import numpy as np
        H = 16
        DH = 64
        M = 32
        ITERS = 6
        K = 13

        def moore_penrose_inverse(a, iters=ITERS):
            a_abs = jnp.abs(a)
            col = a_abs.sum(axis=-1)
            row = a_abs.sum(axis=-2)
            z = jnp.swapaxes(a, -1, -2) / (jnp.max(col) * jnp.max(row))
            I = jnp.eye(a.shape[-1], dtype=a.dtype)
            for _ in range(iters):
                az = a @ z
                z = 0.25 * z @ (13 * I - az @ (15 * I - az @ (7 * I - az)))
            return z
        key = jax.random.key(seed)
        k1, k2, k3, k4 = jax.random.split(key, 4)
        b, n, dim = (4, 512, 128)
        inner = H * DH
        x = jax.random.normal(k1, (b, n, dim), dtype=jnp.float32)
        w_qkv = jax.random.normal(k2, (dim, 3 * inner), dtype=jnp.float32) * 0.02
        w_conv = jax.random.normal(k3, (H, 1, K, 1), dtype=jnp.float32) * 0.1
        w_fc = jax.random.normal(k4, (inner, dim), dtype=jnp.float32) * 0.02
        b_fc = jnp.zeros((dim,), dtype=jnp.float32)
        return {'x': x, 'w_qkv': w_qkv, 'w_conv': w_conv, 'w_fc': w_fc, 'b_fc': b_fc}
    _L0_attn_all = _L0_attn_setup()
    _L0_attn_in = {k: v for k, v in _L0_attn_all.items() if k in ('w_qkv', 'w_conv', 'w_fc', 'b_fc')}
    del _L0_attn_all

    def _L0_xattn_setup():
        import jax, jax.numpy as jnp
        import numpy as np
        E, T, H, F = (8, 256, 128, 512)
        key = jax.random.key(seed)
        k1, k2, k3 = jax.random.split(key, 3)
        x = jax.random.normal(k1, (E, T, H), dtype=jnp.float32)
        w1 = jax.random.normal(k2, (E, F, H), dtype=jnp.float32) * 0.02
        w2 = jax.random.normal(k3, (E, F, H), dtype=jnp.float32) * 0.02
        return {'x': x, 'w1': w1, 'w2': w2}
    _L0_xattn_all = _L0_xattn_setup()
    _L0_xattn_in = {k: v for k, v in _L0_xattn_all.items() if k in ()}
    del _L0_xattn_all

    def _L0_ffn_setup():
        import jax, jax.numpy as jnp
        import numpy as np
        NUM_EXPERTS = 8
        N_EMBD = 128
        D_FF = 4 * N_EMBD
        B, S = (4, 256)
        key = jax.random.key(seed)
        ks = jax.random.split(key, 6)
        x = jax.random.normal(ks[0], (B, S, N_EMBD), dtype=jnp.float32)
        gate_w = jax.random.normal(ks[1], (N_EMBD, NUM_EXPERTS), dtype=jnp.float32) * 0.02
        w1 = jax.random.normal(ks[2], (NUM_EXPERTS, N_EMBD, D_FF), dtype=jnp.float32) * 0.02
        b1 = jnp.zeros((NUM_EXPERTS, D_FF), dtype=jnp.float32)
        w2 = jax.random.normal(ks[3], (NUM_EXPERTS, D_FF, N_EMBD), dtype=jnp.float32) * 0.02
        b2 = jnp.zeros((NUM_EXPERTS, N_EMBD), dtype=jnp.float32)
        return {'x': x, 'gate_w': gate_w, 'w1': w1, 'b1': b1, 'w2': w2, 'b2': b2}
    _L0_ffn_all = _L0_ffn_setup()
    _L0_ffn_in = {k: v for k, v in _L0_ffn_all.items() if k in ('gate_w', 'w1', 'b1', 'w2', 'b2')}
    del _L0_ffn_all
    return {'x': x, 'ctx_1024': ctx_1024, 'L0_attn_w_qkv': _L0_attn_in['w_qkv'], 'L0_attn_w_conv': _L0_attn_in['w_conv'], 'L0_attn_w_fc': _L0_attn_in['w_fc'], 'L0_attn_b_fc': _L0_attn_in['b_fc'], 'L0_ffn_gate_w': _L0_ffn_in['gate_w'], 'L0_ffn_w1': _L0_ffn_in['w1'], 'L0_ffn_b1': _L0_ffn_in['b1'], 'L0_ffn_w2': _L0_ffn_in['w2'], 'L0_ffn_b2': _L0_ffn_in['b2']}

def reference(x, ctx_1024, L0_attn_w_qkv, L0_attn_w_conv, L0_attn_w_fc, L0_attn_b_fc, L0_ffn_gate_w, L0_ffn_w1, L0_ffn_b1, L0_ffn_w2, L0_ffn_b2):
    import jax
    import jax.numpy as jnp

    def _L0_attn_ref(x, w_qkv, w_conv, w_fc, b_fc):
        import jax, jax.numpy as jnp
        import numpy as np
        H = 16
        DH = 64
        M = 32
        ITERS = 6
        K = 13

        def moore_penrose_inverse(a, iters=ITERS):
            a_abs = jnp.abs(a)
            col = a_abs.sum(axis=-1)
            row = a_abs.sum(axis=-2)
            z = jnp.swapaxes(a, -1, -2) / (jnp.max(col) * jnp.max(row))
            I = jnp.eye(a.shape[-1], dtype=a.dtype)
            for _ in range(iters):
                az = a @ z
                z = 0.25 * z @ (13 * I - az @ (15 * I - az @ (7 * I - az)))
            return z
        b, n, dim = x.shape
        scale = DH ** (-0.5)
        qkv = x @ w_qkv
        q, k, v = jnp.split(qkv, 3, axis=-1)
        split_heads = lambda t: t.reshape(b, n, H, DH).transpose(0, 2, 1, 3)
        q, k, v = (split_heads(q) * scale, split_heads(k), split_heads(v))
        l = n // M
        q_l = q.reshape(b, H, M, l, DH).sum(axis=3) / l
        k_l = k.reshape(b, H, M, l, DH).sum(axis=3) / l
        sim1 = jnp.einsum('bhid,bhjd->bhij', q, k_l)
        sim2 = jnp.einsum('bhid,bhjd->bhij', q_l, k_l)
        sim3 = jnp.einsum('bhid,bhjd->bhij', q_l, k)
        attn1 = jax.nn.softmax(sim1, axis=-1)
        attn2 = jax.nn.softmax(sim2, axis=-1)
        attn3 = jax.nn.softmax(sim3, axis=-1)
        attn2_inv = moore_penrose_inverse(attn2)
        out = attn1 @ attn2_inv @ (attn3 @ v)
        res = jax.lax.conv_general_dilated(out, w_conv, window_strides=(1, 1), padding=((K // 2, K // 2), (0, 0)), feature_group_count=H, dimension_numbers=('NCHW', 'OIHW', 'NCHW'))
        out = out + res
        out = out.transpose(0, 2, 1, 3).reshape(b, n, H * DH)
        out = out @ w_fc + b_fc
        return out

    def _L0_xattn_ref(x, w1, w2):
        import jax, jax.numpy as jnp
        import numpy as np
        E, T, H, F = (8, 256, 128, 512)
        h = jnp.einsum('eth,efh->etf', x, w1)
        a = jax.nn.gelu(h, approximate=True)
        return jnp.einsum('etf,efh->eth', a, w2)

    def _L0_ffn_ref(x, gate_w, w1, b1, w2, b2):
        import jax, jax.numpy as jnp
        import numpy as np
        NUM_EXPERTS = 8
        N_EMBD = 128
        D_FF = 4 * N_EMBD
        B, S = (4, 256)
        Bb, Ss, D = x.shape
        x_flat = x.reshape(-1, D)
        router_logits = x_flat @ gate_w
        router_probs = jax.nn.softmax(router_logits, axis=-1)
        expert_idx = jnp.argmax(router_probs, axis=-1)
        expert_w = jnp.take_along_axis(router_probs, expert_idx[:, None], axis=1)[:, 0]
        out = jnp.zeros_like(x_flat)
        for e in range(NUM_EXPERTS):
            h = jax.nn.gelu(x_flat @ w1[e] + b1[e], approximate=False)
            y = h @ w2[e] + b2[e]
            sel = expert_idx == e
            out = out + jnp.where(sel, expert_w, 0.0)[:, None] * y
        return out.reshape(Bb, Ss, D)
    x = _layernorm(x + _L0_attn_ref(x, L0_attn_w_qkv, L0_attn_w_conv, L0_attn_w_fc, L0_attn_b_fc), axis=-1)
    x = _layernorm(x + _L0_xattn_ref(x, ctx_1024, ctx_1024), axis=-1)
    x = _layernorm(x + _L0_ffn_ref(x, L0_ffn_gate_w, L0_ffn_w1, L0_ffn_b1, L0_ffn_w2, L0_ffn_b2), axis=-1)
    return x

_drawn_inputs = setup_inputs


def setup_inputs(seed=0):
    import zlib

    import numpy as np

    out = dict(_drawn_inputs(seed))
    spreads = {'L0_attn_b_fc': (0.0, 0.1), 'L0_ffn_b1': (0.0, 0.8), 'L0_ffn_b2': (0.0, 0.474)}
    factors = {'L0_attn_w_qkv': 3.92,
     'L0_attn_w_conv': 8.0,
     'L0_attn_w_fc': 3.918,
     'L0_ffn_gate_w': 3.067,
     'L0_ffn_w1': 6.172,
     'L0_ffn_w2': 5.602}
    for name, (base, spread) in spreads.items():
        noise = np.random.default_rng([zlib.crc32(name.encode()), seed]).standard_normal(out[name].shape)
        drawn = base * np.exp(spread * noise) if base else spread * noise
        out[name] = jnp.asarray(drawn.astype(out[name].dtype))
    for name, factor in factors.items():
        out[name] = (out[name] * factor).astype(out[name].dtype)
    return out
```

```python
from contextlib import ExitStack

import concourse.bass as bass
from concourse import mybir

F32 = mybir.dt.float32
ALU = mybir.AluOpType
ACT = mybir.ActivationFunctionType
AX_X = mybir.AxisListType.X

P = 128
B, N, D = 8, 128, 128
H, DH = 16, 64
M = 32
L = N // M
ITERS = 6
K = 13
S = 77
E, F = 8, 512
FK = F // P
PAIRS = H // 2
HG = H // 4
GROUPS = B * HG
CH = 4
GC = GROUPS // CH
EPS = 1e-5
BANK = 512


def cubic_factors():
    r = 4.0
    for _ in range(60):
        r -= (((r - 7) * r + 15) * r - 13) / ((3 * r - 14) * r + 15)
    return r, r - 7, 13 / r


ROOT, QB, QA = cubic_factors()


def program(nc, x, ctx_in, w_qkv, w_conv, w_fc, b_fc, gate_w, w1, b1, w2, b2, out):
    ctx = ExitStack()
    with ctx:
        def sb(name, shape):
            return ctx.enter_context(nc.sbuf_tensor(name, shape, F32))

        def sem(name):
            return ctx.enter_context(nc.semaphore(name))

        bank = [ctx.enter_context(nc.psum_tensor(f"bank{i}", [P, BANK], F32)) for i in range(8)]

        ident = sb("ident", [P, P])
        eye_a = sb("eye_a", [P, M])
        ones = sb("ones", [1, P])
        x_sb = sb("x_sb", [P, B, D])
        xT = sb("xT", [P, B * N])
        xl = sb("xl", [P, B * M])
        wqkv = sb("wqkv", [P, 3 * H * DH])
        WT = sb("WT", [P, 3, PAIRS, D])
        wfc = sb("wfc", [P, PAIRS, D])
        NV = sb("NV", [P, H, D])
        qkl = sb("qkl", [P, PAIRS, 2, B * M])
        GG = sb("GG", [P, B, 2, H, M])
        A1 = sb("A1", [P, B, H, M])
        E3 = sb("E3", [P, B, HG, N])
        E3T = sb("E3T", [P, 2, BANK])
        YT = sb("YT", [P, 2, BANK])
        A2 = sb("A2", [P, GROUPS, M])
        A2T = sb("A2T", [P, GROUPS, M])
        V = sb("V", [P, GROUPS, 2, M])
        MM = sb("MM", [P, GROUPS, 2, M])
        QQ = sb("QQ", [P, GROUPS, M])
        GB = sb("GB", [P, GROUPS, M])
        Tt = sb("Tt", [P, H, N])
        taps = sb("taps", [H, K])
        tapr = sb("tapr", [H, 2 * P - 1])
        ctxn = sb("ctxn", [S, B, D])
        ctxT = sb("ctxT", [P, B, S])
        bfc = sb("bfc", [P, D])
        xb = sb("xb", [P, B, D])
        gw = sb("gw", [P, E])
        w1s = sb("w1s", [P, E, F])
        b1n = sb("b1n", [E * FK, P])
        b1T = sb("b1T", [P, E * FK])
        b2s = sb("b2s", [E, D])
        st = sb("st", [P, 1024])
        prio = sb("prio", [P, E])

        gg_flat = GG[:].rearrange("p b w h m -> p (b w h m)")
        CC = gg_flat[:, 0:4096].rearrange("p (b h m) -> p b h m", b=B, h=H)
        U = gg_flat[:, 4096:8192].rearrange("p (b g d) -> p b g d", b=B, g=HG)
        CT = A1[:].rearrange("p b h m -> p (b h m)").rearrange("p (b g n) -> p b g n", b=B, g=HG)
        xTr = GB[:].rearrange("p g m -> p (g m)").rearrange("p (b n) -> p b n", b=B)
        R = E3
        v_flat = V[:].rearrange("p g w m -> p (g w m)")
        gx = v_flat[0:S, 0:1024].rearrange("p (b n) -> p b n", b=B)
        cwT = v_flat[0:E, 1024:2048]
        w2s = E3[:].rearrange("p b g n -> p (b g n)").rearrange("p (e k d) -> p e k d", e=E, k=FK)
        y = wqkv[:, 0:1024].rearrange("p (b d) -> p b d", b=B)
        x1 = wqkv[:, 1024:2048].rearrange("p (b d) -> p b d", b=B)
        xTn = wqkv[:, 2048:3072]
        x2 = xb
        acc = MM[:].rearrange("p g w m -> p (g w m)")[:, 0:1024].rearrange("p (b d) -> p b d", b=B)
        fin = MM[:].rearrange("p g w m -> p (g w m)")[:, 1024:2048].rearrange("p (b d) -> p b d", b=B)
        hT = [qkl[:].rearrange("p a w c -> p (a w c)").rearrange("p (k t) -> p k t", k=FK),
              gg_flat[:, 0:4096].rearrange("p (k t) -> p k t", k=FK)]

        in_x, in_wq, in_wk, in_wv = sem("in_x"), sem("in_wq"), sem("in_wk"), sem("in_wv")
        in_wfc, in_ctx, in_taps, in_bfc = sem("in_wfc"), sem("in_ctx"), sem("in_taps"), sem("in_bfc")
        in_ffn, in_b1, taps_out, in_T = sem("in_ffn"), sem("in_b1"), sem("taps_out"), sem("in_T")
        out_done = sem("out_done")
        zero_done, ident_ready, const_ready = sem("zero_done"), sem("ident_ready"), sem("const_ready")
        taps_zero, taps_rev, taps_ready, xb_ready = (sem("taps_zero"), sem("taps_rev"), sem("taps_ready"),
                                                     sem("xb_ready"))
        ve, ac = sem("vector_step"), sem("scalar_step")
        xT_mm, xT_ready, xl_ready = sem("xT_mm"), sem("xT_ready"), sem("xl_ready")
        xTr_ready = sem("xTr_ready")
        qkl_mm, qkl_even, qkl_odd = sem("qkl_mm"), sem("qkl_even"), sem("qkl_odd")
        sim2_mm, sim2_shift, sim2_exp = sem("sim2_mm"), sem("sim2_shift"), sem("sim2_exp")
        A2_ready, A2T_ready = sem("A2_ready"), sem("A2T_ready")
        WT_mm, WT_ready = sem("WT_mm"), sem("WT_ready")
        GG_mm, GG_even, GG_odd = sem("GG_mm"), sem("GG_even"), sem("GG_odd")
        peak_ready, peak_mm, cinv_ready, c_mm, c_ready = (sem("peak_ready"), sem("peak_mm"), sem("cinv_ready"),
                                                          sem("c_mm"), sem("c_ready"))
        P0_mm, P0_ready = sem("P0_mm"), sem("P0_ready")
        ctxT_mm, ctxT_ready, b1T_mm, b1T_ready = sem("ctxT_mm"), sem("ctxT_ready"), sem("b1T_mm"), sem("b1T_ready")
        NV_mm, NV_ready = sem("NV_mm"), sem("NV_ready")
        sim1_mm, sim1_shift, exp1_done, rsum1, A1_ready = (sem("sim1_mm"), sem("sim1_shift"), sem("exp1_done"),
                                                           sem("rsum1"), sem("A1_ready"))
        sim3_mm, max3_ready, exp3_done, rsum3, attn3_ready = (sem("sim3_mm"), sem("max3_ready"), sem("exp3_done"),
                                                              sem("rsum3"), sem("attn3_ready"))
        E3T_mm, E3T_ready, YT_mm, YT_ready = sem("E3T_mm"), sem("E3T_ready"), sem("YT_mm"), sem("YT_ready")
        R_mm, R_ready = sem("R_mm"), sem("R_ready")
        C_mm, C_even, C_odd = sem("C_mm"), sem("C_even"), sem("C_odd")
        CT_mm, CT_even, CT_odd = sem("CT_mm"), sem("CT_even"), sem("CT_odd")
        PV_mm, MQ_ready, QM_mm, V_ready = sem("PV_mm"), sem("MQ_ready"), sem("QM_mm"), sem("V_ready")
        U_mm, U_even, U_odd = sem("U_mm"), sem("U_even"), sem("U_odd")
        attn_mm, var_ready, std_ready, x1_ready = sem("attn_mm"), sem("var_ready"), sem("std_ready"), sem("x1_ready")
        x1T_mm, x1T_ready, cs_mm, gx_ready, xa_mm = (sem("x1T_mm"), sem("x1T_ready"), sem("cs_mm"), sem("gx_ready"),
                                                     sem("xa_mm"))
        x2_ready, x2T_mm, x2T_ready = sem("x2_ready"), sem("x2T_mm"), sem("x2T_ready")
        gate_mm, gate_shift, gate_exp, cw_ready = sem("gate_mm"), sem("gate_shift"), sem("gate_exp"), sem("cw_ready")
        cwT_mm, cwT_ready, b2_mm = sem("cwT_mm"), sem("cwT_ready"), sem("b2_mm")
        up_mm, h_ready, down_mm, acc_done, fin_ready = (sem("up_mm"), sem("h_ready"), sem("down_mm"),
                                                        sem("acc_done"), sem("fin_ready"))

        padded = nc.dram_tensor("padded_taps", (H, 2 * P - 1), F32)
        toeplitz = bass.AP(padded, 0, [[1, P], [2 * P - 1, H], [1, N]])

        cols = {}
        at = 0
        for name, n in (("mx2", GROUPS), ("rs2", GROUPS), ("cs", GROUPS), ("rows", GROUPS), ("peak", 2), ("pk", 2),
                        ("prod", 1), ("cinv", 1), ("c", 1), ("mx1", B * H), ("rs1", B * H), ("nm3", B * HG),
                        ("s3", B * HG), ("r3", B * HG), ("bn", 6 * B), ("mv", 2 * B), ("sd", B), ("rstd", B),
                        ("gmx", B), ("grs", B), ("gp", B * E), ("gpm", B), ("gsm", B), ("cw", B * E),
                        ("gm", B * E)):
            cols[name] = (at, n)
            at += n

        def stat(name, lo=0, n=None):
            a, k = cols[name]
            return st[:, a + lo:a + lo + (k if n is None else n)]

        def quad(q):
            return slice(M * q, M * (q + 1))

        block = ctx.enter_context(nc.Block())

        @block.sync
        def _(sp):
            sp.dma_start(x_sb[:], x.rearrange("b n d -> n b d")).then_inc(in_x, 16)
            sp.dma_start(wqkv[:, 0:1024], w_qkv[:, 0:1024]).then_inc(in_wq, 16)
            sp.dma_start(wqkv[:, 1024:2048], w_qkv[:, 1024:2048]).then_inc(in_wk, 16)
            sp.dma_start(wqkv[:, 2048:3072], w_qkv[:, 2048:3072]).then_inc(in_wv, 16)
            sp.dma_start(taps[:], w_conv.rearrange("h a k b -> h (a k b)")).then_inc(in_taps, 16)
            sp.dma_start(wfc[:], w_fc.rearrange("(p c) d -> c p d", c=P)).then_inc(in_wfc, 16)
            sp.dma_start(ctxn[:], ctx_in.rearrange("b s d -> s b d")).then_inc(in_ctx, 16)
            sp.dma_start(bfc[:], b_fc.rearrange("(a d) -> a d", a=1).broadcast_to([P, D])).then_inc(in_bfc, 16)
            sp.dma_start(b1n[:], b1.rearrange("e (k p) -> (e k) p", k=FK)).then_inc(in_b1, 16)
            sp.wait_ge(taps_ready, 1)
            sp.dma_start(padded.ap(), tapr[:]).then_inc(taps_out, 16)
            sp.wait_ge(taps_out, 16)
            sp.dma_start(Tt[:], toeplitz).then_inc(in_T, 16)
            sp.dma_start(gw[:], gate_w).then_inc(in_ffn, 16)
            sp.dma_start(b2s[:], b2).then_inc(in_ffn, 16)
            sp.dma_start(w1s[:], w1.rearrange("e d f -> d e f")).then_inc(in_ffn, 16)
            sp.wait_ge(U_mm, B)
            sp.dma_start(w2s, w2.rearrange("e (k p) d -> p e k d", k=FK)).then_inc(in_ffn, 16)
            sp.wait_ge(fin_ready, B)
            sp.dma_start(out.rearrange("b n d -> n b d"), fin).then_inc(out_done, 16)
            sp.wait_ge(out_done, 16)

        @block.gpsimd
        def _(pool):
            nc.gpsimd.memset(ident[:], 0.0).then_inc(zero_done, 1)
            pool.wait_ge(zero_done, 1)
            nc.gpsimd.affine_select(out=ident[:], in_=ident[:], compare_op=ALU.not_equal, fill=1.0, base=0,
                                    pattern=[[-1, P]], channel_multiplier=1).then_inc(ident_ready, 1)
            nc.gpsimd.memset(tapr[:], 0.0).then_inc(taps_zero, 1)
            nc.gpsimd.memset(ones[:], 1.0).then_inc(const_ready, 1)
            for e in range(E):
                nc.gpsimd.memset(prio[:, e:e + 1], float(E - e)).then_inc(const_ready, 1)
            pool.wait_ge(taps_zero, 1)
            pool.wait_ge(in_taps, 16)
            first = P - 1 - K // 2
            nc.gpsimd.tensor_copy(tapr[:, first:first + K], taps[:, ::-1]).then_inc(taps_rev, 1)
            pool.wait_ge(taps_rev, 1)
            nc.gpsimd.tensor_scalar(tapr[:, P - 1:P], tapr[:, P - 1:P], 1.0, None, ALU.add).then_inc(taps_ready, 1)
            pool.wait_ge(ident_ready, 1)
            for q in range(4):
                eye = ident[quad(q), quad(q)]
                nc.gpsimd.tensor_scalar(eye_a[quad(q), :], eye, QA, None, ALU.mult).then_inc(const_ready, 1)
            pool.wait_ge(const_ready, 1 + E + 4)
            pool.wait_ge(xT_ready, 2)
            nc.gpsimd.tensor_copy(xTr, xT[:].rearrange("p (b n) -> p b n", b=B)[:, :, ::-1]).then_inc(xTr_ready, 1)
            pool.wait_ge(in_bfc, 16)
            nc.gpsimd.tensor_tensor(xb[:], x_sb[:], bfc[:].unsqueeze(1).broadcast_to([P, B, D]), ALU.add
                                    ).then_inc(xb_ready, 1)
            for b in range(B):
                pool.wait_ge(rsum3, b + 1)
                nc.gpsimd.tensor_tensor(E3[:, b], E3[:, b], stat("r3", HG * b, HG).unsqueeze(2)
                                        .broadcast_to([P, HG, N]), ALU.mult).then_inc(attn3_ready, 1)
                pool.wait_ge(rsum1, b + 1)
                nc.gpsimd.tensor_tensor(A1[:, b], A1[:, b], stat("rs1", H * b, H).unsqueeze(2)
                                        .broadcast_to([P, H, M]), ALU.mult).then_inc(A1_ready, 1)

        @block.tensor
        def _(pe):
            mm, tr = nc.tensor.matmul, nc.tensor.transpose
            pe.wait_ge(ident_ready, 1)
            pe.wait_ge(in_x, 16)
            for b in range(B):
                i = tr(bank[b // 4][:, P * (b % 4):P * (b % 4 + 1)], x_sb[:, b, :], ident[:])
                if b % 4 == 3:
                    i.then_inc(xT_mm, 1)
            pe.wait_ge(xl_ready, 1)
            pe.wait_ge(in_wq, 16)
            pe.wait_ge(in_wk, 16)
            for p in range(PAIRS):
                for w in range(2):
                    i = mm(bank[(2 + p) % 8][:, 256 * w:256 * w + 256], wqkv[:, 1024 * w + P * p:1024 * w + P * p + P],
                           xl[:], start=True, stop=True)
                i.then_inc(qkl_mm, 1)
            pe.wait_ge(qkl_even, PAIRS // 2)
            pe.wait_ge(qkl_odd, PAIRS // 2)
            for b in range(B):
                for h in range(H):
                    k = slice(DH * (h % 2), DH * (h % 2) + DH)
                    c = ((b % 4) * HG + h // 4) * M
                    i = mm(bank[2 + b // 4][quad(h % 4), c:c + M], qkl[k, h // 2, 0, M * b:M * b + M],
                           qkl[k, h // 2, 1, M * b:M * b + M], start=True, stop=True)
                if b % 4 == 3:
                    i.then_inc(sim2_mm, 1)
            for n in range(3 * PAIRS):
                if n == 2 * PAIRS:
                    pe.wait_ge(in_wv, 16)
                i = tr(bank[(4 + n // 4) % 8][:, P * (n % 4):P * (n % 4) + P], wqkv[:, P * n:P * n + P], ident[:])
                if n % 4 == 3:
                    i.then_inc(WT_mm, 1)
            pe.wait_ge(WT_ready, 6)
            for h in range(H):
                if h < 2:
                    pe.wait_ge(sim2_shift, h + 1)
                if h >= 8:
                    pe.wait_ge(GG_even if h % 2 == 0 else GG_odd, (h - 8) // 2 + 1)
                k = slice(DH * (h % 2), DH * (h % 2) + DH)
                mm(bank[(2 + h) % 8][:, 0:256], WT[k, 0, h // 2, :], qkl[k, h // 2, 1, :], start=True, stop=True)
                mm(bank[(2 + h) % 8][:, 256:512], WT[k, 1, h // 2, :], qkl[k, h // 2, 0, :],
                   start=True, stop=True).then_inc(GG_mm, 1)
            pe.wait_ge(in_wfc, 16)
            pe.wait_ge(GG_odd, 7)
            pe.wait_ge(GG_even, 8)
            for p in range(PAIRS):
                for w in range(2):
                    k = slice(DH * w, DH * w + DH)
                    c = P * (p % 4)
                    i = mm(bank[(5 + p // 4 + 2 * w) % 8][:, c:c + P], WT[k, 2, p, :], wfc[k, p, :],
                           start=True, stop=True)
                if p % 4 == 3:
                    i.then_inc(NV_mm, 1)
            pe.wait_ge(in_ctx, 16)
            pe.wait_ge(GG_odd, 8)
            pe.wait_ge(in_b1, 16)
            for b in range(B):
                i = tr(bank[1][:, S * (b % 4):S * (b % 4) + S], ctxn[:, b, :], ident[0:S, 0:S])
                if b == 3:
                    i.then_inc(ctxT_mm, 1)
                    pe.wait_ge(ctxT_ready, 1)
            i.then_inc(ctxT_mm, 1)
            pe.wait_ge(ctxT_ready, 2)
            tr(bank[1][:, 0:E * FK], b1n[:], ident[0:E * FK, 0:E * FK]).then_inc(b1T_mm, 1)
            pe.wait_ge(peak_ready, 1)
            for w in range(2):
                i = tr(bank[2][0:1, P * w:P * w + P], stat("peak", w, 1), ident[:])
            i.then_inc(peak_mm, 1)
            pe.wait_ge(const_ready, 1)
            pe.wait_ge(cinv_ready, 1)
            mm(bank[2][:, 256:257], ones[:], stat("cinv")[0:1, :], start=True, stop=True).then_inc(c_mm, 1)
            pe.wait_ge(A2T_ready, 1)
            for g in range(GROUPS):
                for q in range(4):
                    t = A2T[quad(q), g, :]
                    i = mm(bank[3 + g // 16][quad(q), M * (g % 16):M * (g % 16) + M], t, t, start=True, stop=True)
                if g % 16 == 15:
                    i.then_inc(P0_mm, 1)
            pe.wait_ge(b1T_ready, 1)
            pe.wait_ge(c_ready, 1)
            pe.wait_ge(NV_ready, 2)
            pe.wait_ge(P0_ready, 4)
            pe.wait_ge(xTr_ready, 1)
            for s in range(B + 4):
                if s < B:
                    if s >= 2:
                        pe.wait_ge(sim1_shift, s - 1)
                    mm(bank[1 + s % 2][:], xTr[:, s, :], GG[:, s, 0].rearrange("p h m -> p (h m)"),
                       start=True, stop=True).then_inc(sim1_mm, 1)
                    if s >= 2:
                        pe.wait_ge(exp3_done, HG * (s - 1))
                    for g in range(HG):
                        i = mm(bank[5 + s % 2][:, N * g:N * g + N], GG[:, s, 1, 4 * g:4 * g + 4].rearrange("p h m -> p (h m)"),
                               xT[:, N * s:N * s + N], start=True, stop=True)
                    i.then_inc(sim3_mm, 1)
                if 2 <= s < B + 2:
                    b = s - 2
                    pe.wait_ge(attn3_ready, b + 1)
                    if b >= 1:
                        pe.wait_ge(E3T_ready, b)
                    for g in range(HG):
                        i = tr(bank[7][:, P * g:P * g + P], E3[:, b, g, :], ident[:])
                    i.then_inc(E3T_mm, 1)
                if 3 <= s < B + 3:
                    b = s - 3
                    pe.wait_ge(E3T_ready, b + 1)
                    if b >= 1:
                        pe.wait_ge(YT_ready, b)
                    mm(bank[0][:], x_sb[:, b, :], E3T[:, b % 2, :], start=True, stop=True).then_inc(YT_mm, 1)
                if s >= 4:
                    b = s - 4
                    pe.wait_ge(YT_ready, b + 1)
                    if b >= 2:
                        pe.wait_ge(R_ready, b - 1)
                    for h in range(H):
                        i = mm(bank[3 + b % 2][quad(h % 4), P * (h // 4):P * (h // 4) + P],
                               YT[:, b % 2, M * h:M * h + M], NV[:, h, :], start=True, stop=True)
                    i.then_inc(R_mm, 1)
            pe.wait_ge(A1_ready, B)
            pe.wait_ge(in_T, 16)
            pe.wait_ge(R_ready, B)
            for p in range(PAIRS):
                for w in range(2):
                    i = mm(bank[p][:, 256 * w:256 * w + 256], Tt[:, 2 * p + w, :], A1[:, :, 2 * p + w, :],
                           start=True, stop=True)
                i.then_inc(C_mm, 1)
            pe.wait_ge(C_even, 4)
            pe.wait_ge(C_odd, 4)
            for b in range(B):
                for g in range(HG):
                    i = tr(bank[b][:, N * g:N * g + N], CC[:, b, 4 * g:4 * g + 4].rearrange("p h m -> p (h m)"), ident[:])
                i.then_inc(CT_mm, 1)
            pe.wait_ge(CT_even, 4)
            pe.wait_ge(CT_odd, 4)
            pe.wait_ge(const_ready, 1 + E + 4)
            steps = ITERS * CH
            for k in range(steps + 2):
                if k < steps:
                    c = k % CH
                    if k >= CH:
                        pe.wait_ge(V_ready, k - CH + 1)
                    if k >= 2:
                        pe.wait_ge(MQ_ready, 2 * (k - 1))
                    for g in range(GC):
                        for q in range(4):
                            v = V[quad(q), GC * c + g]
                            i = mm(bank[c % 2][quad(q), 64 * g:64 * g + 64], v[:, 0, :], v, start=True, stop=True)
                    i.then_inc(PV_mm, 1)
                if k >= 2:
                    j = k - 2
                    c, last = j % CH, j >= steps - CH
                    pe.wait_ge(MQ_ready, 2 * (j + 1))
                    if j >= 2:
                        pe.wait_ge(V_ready, j - 1)
                    for g in range(GC):
                        for q in range(4):
                            m = MM[quad(q), GC * c + g, 1 if last else 0:2, :]
                            w = 32 * last
                            i = mm(bank[2 + c % 2][quad(q), 64 * g + w:64 * g + 64], QQ[quad(q), GC * c + g, :], m,
                                   start=True, stop=True)
                    i.then_inc(QM_mm, 1)
            for b in range(B):
                if b % 2 == 0:
                    pe.wait_ge(V_ready, steps - CH + b // 2 + 1)
                if b >= 4:
                    pe.wait_ge(U_even if b % 2 == 0 else U_odd, (b - 4) // 2 + 1)
                for g in range(HG):
                    for q in range(4):
                        i = mm(bank[4 + b % 4][quad(q), D * g:D * g + D], V[quad(q), HG * b + g, 1, :], R[quad(q), b, g, :],
                               start=True, stop=True)
                i.then_inc(U_mm, 1)
            for b in range(B):
                pe.wait_ge(U_even if b % 2 == 0 else U_odd, b // 2 + 1)
                for g in range(HG):
                    i = mm(bank[b // 4][:, D * (b % 4):D * (b % 4) + D], CT[:, b, g, :], U[:, b, g, :],
                           start=(g == 0), stop=(g == HG - 1))
                if b % 4 == 3:
                    i.then_inc(attn_mm, 1)
            for b in range(B):
                pe.wait_ge(x1_ready, b + 1)
                i = tr(bank[b // 4][:, N * (b % 4):N * (b % 4) + N], x1[:, b, :], ident[:])
                if b % 4 == 3:
                    i.then_inc(x1T_mm, 1)
            for b in range(B):
                pe.wait_ge(x1T_ready, b // 4 + 1)
                i = mm(bank[2 + b // 4][0:S, N * (b % 4):N * (b % 4) + N], ctxT[:, b, :], xTn[:, N * b:N * b + N],
                       start=True, stop=True)
                if b % 4 == 3:
                    i.then_inc(cs_mm, 1)
            for b in range(B):
                pe.wait_ge(gx_ready, b // 4 + 1)
                i = mm(bank[4 + b // 4][:, D * (b % 4):D * (b % 4) + D], gx[:, b, :], ctxn[:, b, :],
                       start=True, stop=True)
                if b % 4 == 3:
                    i.then_inc(xa_mm, 1)
            for b in range(B):
                pe.wait_ge(x2_ready, b + 1)
                i = tr(bank[b // 4][:, N * (b % 4):N * (b % 4) + N], x2[:, b, :], ident[:])
                if b % 4 == 3:
                    i.then_inc(x2T_mm, 1)
            pe.wait_ge(in_ffn, 64)
            for b in range(B):
                pe.wait_ge(x2T_ready, b // 4 + 1)
                i = mm(bank[2][:, E * b:E * b + E], xTn[:, N * b:N * b + N], gw[:], start=True, stop=True)
            i.then_inc(gate_mm, 1)

            def up(e):
                for k in range(FK):
                    for t in range(2):
                        n = (e * FK + k) * 2 + t
                        if n >= 4:
                            pe.wait_ge(h_ready, n - 3)
                        mm(bank[n % 4][:], w1s[:, e, P * k:P * k + P], xTn[:, 512 * t:512 * t + 512],
                           start=True, stop=True).then_inc(up_mm, 1)

            def down(e):
                for b in range(B):
                    n = e * 2 + b // 4
                    if b % 4 == 0 and n >= 4:
                        pe.wait_ge(acc_done, 8 + 4 * (n - 3))
                    if b == 0:
                        pe.wait_ge(h_ready, 8 * e + 8)
                    for k in range(FK):
                        i = mm(bank[4 + n % 4][:, D * (b % 4):D * (b % 4) + D], hT[e % 2][:, k, N * b:N * b + N],
                               w2s[:, e, k, :], start=(k == 0), stop=(k == FK - 1))
                    if b % 4 == 3:
                        i.then_inc(down_mm, 1)

            pe.wait_ge(gate_shift, 1)
            up(0)
            pe.wait_ge(cw_ready, 1)
            for b in range(B):
                i = tr(bank[6 + b // 4][0:E, N * (b % 4):N * (b % 4) + N], stat("cw", E * b, E), ident[:])
                if b % 4 == 3:
                    i.then_inc(cwT_mm, 1)
            for b in range(B):
                pe.wait_ge(cwT_ready, b // 4 + 1)
                i = mm(bank[4 + b // 4][:, D * (b % 4):D * (b % 4) + D], cwT[:, N * b:N * b + N], b2s[:],
                       start=True, stop=True)
                if b % 4 == 3:
                    i.then_inc(b2_mm, 1)
            up(1)
            pe.wait_ge(acc_done, 8)
            for e in range(E):
                down(e)
                if e + 2 < E:
                    up(e + 2)

        @block.scalar
        def _(act):
            n_ac = 0
            for p in range(1, PAIRS, 2):
                act.wait_ge(qkl_mm, p + 1)
                nc.scalar.copy(qkl[:, p], bank[(2 + p) % 8][:].rearrange("p (w c) -> p w c", w=2)).then_inc(qkl_odd, 1)
            for n in range(6):
                act.wait_ge(WT_mm, n + 1)
                nc.scalar.copy(WT[:, n // 2, 4 * (n % 2):4 * (n % 2) + 4, :],
                               bank[(4 + n) % 8][:].rearrange("p (a d) -> p a d", a=4)).then_inc(WT_ready, 1)
                if n in (1, 3):
                    i = n // 2
                    act.wait_ge(sim2_shift, i + 1)
                    nc.scalar.activation(A2[:, 16 * i:16 * i + 16], A2[:, 16 * i:16 * i + 16], ACT.Exp,
                                         scale=DH ** -0.5 / L / L).then_inc(sim2_exp, 1)
            for h in range(0, H, 2):
                act.wait_ge(GG_mm, h + 1)
                nc.scalar.copy(GG[:, :, :, h, :].rearrange("p b w m -> p w b m"),
                bank[(2 + h) % 8][:].rearrange("p (w b m) -> p w b m", w=2, b=B)).then_inc(GG_even, 1)
            for n in range(2):
                act.wait_ge(NV_mm, n + 1)
                for w in range(2):
                    i = nc.scalar.copy(NV[:, 8 * n + w:8 * n + 8:2, :],
                                       bank[(5 + n + 2 * w) % 8][:].rearrange("p (a d) -> p a d", a=4))
                    i.then_inc(NV_ready if w else ac, 1)
            for n in range(2):
                act.wait_ge(ctxT_mm, n + 1)
                nc.scalar.copy(ctxT[:, 4 * n:4 * n + 4, :], bank[1][:, 0:4 * S].rearrange("p (a s) -> p a s", a=4)
                               ).then_inc(ctxT_ready, 1)
            act.wait_ge(b1T_mm, 1)
            nc.scalar.copy(b1T[:], bank[1][:, 0:E * FK]).then_inc(b1T_ready, 1)
            act.wait_ge(c_ready, 1)
            for n in range(2):
                act.wait_ge(P0_mm, n + 1)
                nc.scalar.activation(V[:, 16 * n:16 * n + 16, 0, :], bank[3 + n][:].rearrange("p (g m) -> p g m", g=16),
                                     ACT.Copy, scale=stat("c")).then_inc(P0_ready, 1)
                nc.scalar.activation(V[:, 16 * n:16 * n + 16, 1, :], A2[:, 16 * n:16 * n + 16], ACT.Copy,
                                     scale=stat("c")).then_inc(P0_ready, 1)
            for s in range(B + 4):
                if s < B:
                    act.wait_ge(sim1_shift, s + 1)
                    nc.scalar.activation(A1[:, s], A1[:, s], ACT.Exp, scale=DH ** -0.5 / L).then_inc(exp1_done, 1)
                    act.wait_ge(max3_ready, s + 1)
                    for g in range(HG):
                        nc.scalar.activation(E3[:, s, g, :], bank[5 + s % 2][:, N * g:N * g + N], ACT.Exp,
                                             bias=stat("nm3", HG * s + g, 1), scale=DH ** -0.5 / L,
                                             accum_out=stat("s3", HG * s + g, 1)).then_inc(exp3_done, 1)
                if 3 <= s < B + 3:
                    act.wait_ge(YT_mm, s - 2)
                    nc.scalar.copy(YT[:, (s - 3) % 2, :], bank[0][:]).then_inc(YT_ready, 1)
                if s >= 4:
                    b = s - 4
                    act.wait_ge(R_mm, b + 1)
                    nc.scalar.copy(R[:, b], bank[3 + b % 2][:].rearrange("p (g d) -> p g d", g=HG)).then_inc(R_ready, 1)
            for p in range(1, PAIRS, 2):
                act.wait_ge(C_mm, p + 1)
                nc.scalar.copy(CC[:, :, 2 * p:2 * p + 2].rearrange("p b h m -> p h b m"), bank[p][:].rearrange("p (h b m) -> p h b m", h=2, b=B)
                               ).then_inc(C_odd, 1)
            for b in range(1, B, 2):
                act.wait_ge(CT_mm, b + 1)
                nc.scalar.copy(CT[:, b], bank[b][:].rearrange("p (g n) -> p g n", g=HG)).then_inc(CT_odd, 1)
            steps = ITERS * CH
            for k in range(steps):
                c, last = k % CH, k >= steps - CH
                act.wait_ge(QM_mm, k + 1)
                nc.scalar.mul(V[:, GC * c:GC * c + GC, last:2, :],
                              bank[2 + c % 2][:].rearrange("p (g w m) -> p g w m", g=GC, w=2)[:, :, last:2, :],
                              0.25).then_inc(V_ready, 1)
            for b in range(1, B, 2):
                act.wait_ge(U_mm, b + 1)
                nc.scalar.copy(U[:, b], bank[4 + b % 4][:].rearrange("p (g d) -> p g d", g=HG)).then_inc(U_odd, 1)
            act.wait_ge(var_ready, 1)
            nc.scalar.activation(stat("sd"), stat("sd"), ACT.Sqrt).then_inc(std_ready, 1)
            for n in range(2):
                act.wait_ge(cs_mm, n + 1)
                nc.scalar.activation(gx[:, 4 * n:4 * n + 4, :], bank[2 + n][0:S, :].rearrange("p (b n) -> p b n", b=4),
                                     ACT.Gelu_apprx_tanh).then_inc(gx_ready, 1)
            act.wait_ge(var_ready, 2)
            nc.scalar.activation(stat("sd"), stat("sd"), ACT.Sqrt).then_inc(std_ready, 1)
            act.wait_ge(gate_shift, 1)
            nc.scalar.activation(stat("gp"), stat("gp"), ACT.Exp).then_inc(gate_exp, 1)
            for n in range(E * FK * 2):
                e, k, t = n // 8, n // 2 % FK, n % 2
                act.wait_ge(up_mm, n + 1)
                if e >= 2 and n % 8 == 0:
                    act.wait_ge(down_mm, 2 * (e - 1))
                nc.scalar.activation(hT[e % 2][:, k, 512 * t:512 * t + 512], bank[n % 4][:], ACT.Gelu,
                                     bias=b1T[:, e * FK + k:e * FK + k + 1]).then_inc(h_ready, 1)
            act.wait_ge(var_ready, 3)
            nc.scalar.activation(stat("sd"), stat("sd"), ACT.Sqrt).then_inc(std_ready, 1)

        @block.vector
        def _(dve):
            v = nc.vector
            count = [0]

            def step(ins):
                ins.then_inc(ve, 1)
                count[0] += 1

            def settle():
                dve.wait_ge(ve, count[0])

            for i in range(2):
                dve.wait_ge(xT_mm, i + 1)
                v.tensor_copy(xT[:, BANK * i:BANK * (i + 1)], bank[i][:]).then_inc(xT_ready, 1)
            dve.wait_ge(xT_ready, 2)
            v.tensor_reduce(xl[:], xT[:].rearrange("p (c l) -> p c l", l=L), AX_X, ALU.add).then_inc(xl_ready, 1)
            for p in range(0, PAIRS, 2):
                dve.wait_ge(qkl_mm, p + 1)
                v.tensor_copy(qkl[:, p], bank[(2 + p) % 8][:].rearrange("p (w c) -> p w c", w=2)).then_inc(qkl_even, 1)
            for i in range(2):
                g = slice(16 * i, 16 * i + 16)
                ps = bank[2 + i][:].rearrange("p (g m) -> p g m", g=16)
                dve.wait_ge(sim2_mm, i + 1)
                step(v.tensor_reduce(stat("mx2", 16 * i, 16), ps, AX_X, ALU.max))
                settle()
                v.tensor_tensor(A2[:, g], ps, stat("mx2", 16 * i, 16).unsqueeze(2).broadcast_to([P, 16, M]),
                                ALU.subtract).then_inc(sim2_shift, 1)
            for i in range(2):
                g = slice(16 * i, 16 * i + 16)
                dve.wait_ge(sim2_exp, i + 1)
                step(v.tensor_reduce(stat("rs2", 16 * i, 16), A2[:, g], AX_X, ALU.add))
                settle()
                step(v.reciprocal(stat("rs2", 16 * i, 16), stat("rs2", 16 * i, 16)))
                settle()
                v.tensor_tensor(A2[:, g], A2[:, g], stat("rs2", 16 * i, 16).unsqueeze(2).broadcast_to([P, 16, M]),
                                ALU.mult).then_inc(A2_ready, 1)
            dve.wait_ge(A2_ready, 2)
            v.transpose(A2T[:].rearrange("p g m -> p (g m)"), A2[:].rearrange("p g m -> p (g m)")).then_inc(A2T_ready, 1)
            step(v.tensor_reduce(stat("cs"), A2[:], AX_X, ALU.add))
            dve.wait_ge(A2T_ready, 1)
            step(v.tensor_reduce(stat("rows"), A2T[:], AX_X, ALU.add))
            settle()
            step(v.tensor_reduce(stat("peak", 0, 1), stat("cs"), AX_X, ALU.max))
            v.tensor_reduce(stat("peak", 1, 1), stat("rows"), AX_X, ALU.max).then_inc(peak_ready, 1)
            for h in range(1, H, 2):
                dve.wait_ge(GG_mm, h + 1)
                v.tensor_copy(GG[:, :, :, h, :].rearrange("p b w m -> p w b m"),
                bank[(2 + h) % 8][:].rearrange("p (w b m) -> p w b m", w=2, b=B)).then_inc(GG_odd, 1)
            dve.wait_ge(peak_mm, 1)
            step(v.tensor_reduce(stat("pk")[0:1, :], bank[2][0:1, 0:256].rearrange("p (w n) -> p w n", w=2),
                                 AX_X, ALU.max))
            settle()
            step(v.tensor_tensor(stat("prod")[0:1, :], stat("pk", 0, 1)[0:1, :], stat("pk", 1, 1)[0:1, :], ALU.mult))
            settle()
            v.reciprocal(stat("cinv")[0:1, :], stat("prod")[0:1, :]).then_inc(cinv_ready, 1)
            dve.wait_ge(c_mm, 1)
            v.tensor_copy(stat("c"), bank[2][:, 256:257]).then_inc(c_ready, 1)
            for s in range(B + 3):
                if s < B:
                    ps = bank[1 + s % 2][:].rearrange("p (h m) -> p h m", h=H)
                    dve.wait_ge(sim1_mm, s + 1)
                    step(v.tensor_reduce(stat("mx1", H * s, H), ps, AX_X, ALU.max))
                    dve.wait_ge(sim3_mm, s + 1)
                    step(v.tensor_reduce(stat("nm3", HG * s, HG),
                                         bank[5 + s % 2][:].rearrange("p (g n) -> p g n", g=HG), AX_X, ALU.max))
                    settle()
                    v.tensor_tensor(A1[:, s], ps, stat("mx1", H * s, H).unsqueeze(2).broadcast_to([P, H, M]),
                                    ALU.subtract).then_inc(sim1_shift, 1)
                    v.tensor_scalar(stat("nm3", HG * s, HG), stat("nm3", HG * s, HG), -DH ** -0.5 / L, None,
                                    ALU.mult).then_inc(max3_ready, 1)
                if 3 <= s:
                    b = s - 3
                    dve.wait_ge(E3T_mm, b + 1)
                    if b >= 2:
                        dve.wait_ge(YT_mm, b - 1)
                    v.tensor_copy(E3T[:, b % 2, :], bank[7][:]).then_inc(E3T_ready, 1)
                if 1 <= s < B + 1:
                    b = s - 1
                    dve.wait_ge(exp3_done, HG * (b + 1))
                    v.reciprocal(stat("r3", HG * b, HG), stat("s3", HG * b, HG)).then_inc(rsum3, 1)
                    dve.wait_ge(exp1_done, b + 1)
                    step(v.tensor_reduce(stat("rs1", H * b, H), A1[:, b], AX_X, ALU.add))
                    settle()
                    v.reciprocal(stat("rs1", H * b, H), stat("rs1", H * b, H)).then_inc(rsum1, 1)
            for p in range(0, PAIRS, 2):
                dve.wait_ge(C_mm, p + 1)
                v.tensor_copy(CC[:, :, 2 * p:2 * p + 2].rearrange("p b h m -> p h b m"), bank[p][:].rearrange("p (h b m) -> p h b m", h=2, b=B)
                              ).then_inc(C_even, 1)
            for b in range(0, B, 2):
                dve.wait_ge(CT_mm, b + 1)
                v.tensor_copy(CT[:, b], bank[b][:].rearrange("p (g n) -> p g n", g=HG)).then_inc(CT_even, 1)
            dve.wait_ge(const_ready, 1 + E + 4)
            steps = ITERS * CH
            for k in range(steps):
                c = k % CH
                g = slice(GC * c, GC * c + GC)
                if k >= CH:
                    dve.wait_ge(V_ready, k - CH + 1)
                else:
                    dve.wait_ge(P0_ready, 2 * (c // 2 + 1))
                step(v.scalar_tensor_tensor(out=GB[:, g], in0=V[:, g, 0, :], scalar=QB,
                                            in1=eye_a[:].unsqueeze(1).broadcast_to([P, GC, M]),
                                            op0=ALU.mult, op1=ALU.add))
                dve.wait_ge(PV_mm, k + 1)
                ps = bank[c % 2][:].rearrange("p (g w m) -> p g w m", g=GC, w=2)
                v.scalar_tensor_tensor(out=MM[:, g].rearrange("p g w m -> p (g w m)"),
                                       in0=V[:, g].rearrange("p g w m -> p (g w m)"), scalar=ROOT,
                                       in1=bank[c % 2][:], op0=ALU.mult, op1=ALU.subtract).then_inc(MQ_ready, 1)
                settle()
                v.tensor_tensor(QQ[:, g], GB[:, g], ps[:, :, 0, :], ALU.add).then_inc(MQ_ready, 1)
            for b in range(0, B, 2):
                dve.wait_ge(U_mm, b + 1)
                v.tensor_copy(U[:, b], bank[4 + b % 4][:].rearrange("p (g d) -> p g d", g=HG)).then_inc(U_even, 1)

            def layer_norm(n, src, dst, ready):
                settle()
                for b in range(B):
                    step(v.bn_stats(stat("bn", 6 * b, 6), src[:, b, :]))
                settle()
                for b in range(B):
                    step(v.bn_aggr(stat("mv", 2 * b, 2), stat("bn", 6 * b, 6)))
                settle()
                v.tensor_scalar(stat("sd"), stat("mv").rearrange("p (b w) -> p b w", w=2)[:, :, 1], EPS, None,
                                ALU.add).then_inc(var_ready, 1)
                dve.wait_ge(std_ready, n + 1)
                step(v.reciprocal(stat("rstd"), stat("sd")))
                settle()
                for b in range(B):
                    v.tensor_scalar(dst[:, b, :], src[:, b, :], stat("mv", 2 * b, 1), stat("rstd", b, 1),
                                    ALU.subtract, ALU.mult).then_inc(ready, 1)

            dve.wait_ge(xb_ready, 1)
            for n in range(2):
                dve.wait_ge(attn_mm, n + 1)
                step(v.tensor_tensor(y[:, 4 * n:4 * n + 4, :], xb[:, 4 * n:4 * n + 4, :],
                                     bank[n][:].rearrange("p (b d) -> p b d", b=4), ALU.add))
            layer_norm(0, y, x1, x1_ready)
            for n in range(2):
                dve.wait_ge(x1T_mm, n + 1)
                v.tensor_copy(xTn[:, BANK * n:BANK * n + BANK], bank[n][:]).then_inc(x1T_ready, 1)
            dve.wait_ge(x1_ready, B)
            for n in range(2):
                dve.wait_ge(xa_mm, n + 1)
                step(v.tensor_tensor(y[:, 4 * n:4 * n + 4, :], x1[:, 4 * n:4 * n + 4, :],
                                     bank[4 + n][:].rearrange("p (b d) -> p b d", b=4), ALU.add))
            layer_norm(1, y, x2, x2_ready)
            for n in range(2):
                dve.wait_ge(x2T_mm, n + 1)
                v.tensor_copy(xTn[:, BANK * n:BANK * n + BANK], bank[n][:]).then_inc(x2T_ready, 1)
            be = [P, B, E]
            gl = bank[2][:, 0:B * E].rearrange("p (b e) -> p b e", b=B)
            gp = stat("gp").rearrange("p (b e) -> p b e", b=B)
            gm = stat("gm").rearrange("p (b e) -> p b e", b=B)
            cw = stat("cw").rearrange("p (b e) -> p b e", b=B)
            dve.wait_ge(gate_mm, 1)
            step(v.tensor_reduce(stat("gmx"), gl, AX_X, ALU.max))
            settle()
            v.tensor_tensor(gp, gl, stat("gmx").unsqueeze(2).broadcast_to(be), ALU.subtract).then_inc(gate_shift, 1)
            dve.wait_ge(gate_exp, 1)
            step(v.tensor_reduce(stat("grs"), gp, AX_X, ALU.add))
            settle()
            step(v.reciprocal(stat("grs"), stat("grs")))
            settle()
            step(v.tensor_tensor(gp, gp, stat("grs").unsqueeze(2).broadcast_to(be), ALU.mult))
            settle()
            step(v.tensor_reduce(stat("gpm"), gp, AX_X, ALU.max))
            settle()
            step(v.tensor_tensor(gm, gp, stat("gpm").unsqueeze(2).broadcast_to(be), ALU.is_equal))
            settle()
            step(v.tensor_tensor(gm, gm, prio[:].unsqueeze(1).broadcast_to(be), ALU.mult))
            settle()
            step(v.tensor_reduce(stat("gsm"), gm, AX_X, ALU.max))
            settle()
            step(v.tensor_tensor(gm, gm, stat("gsm").unsqueeze(2).broadcast_to(be), ALU.is_equal))
            settle()
            v.tensor_tensor(cw, gm, stat("gpm").unsqueeze(2).broadcast_to(be), ALU.mult).then_inc(cw_ready, 1)
            for n in range(2):
                dve.wait_ge(cwT_mm, n + 1)
                v.tensor_copy(cwT[:, BANK * n:BANK * n + BANK], bank[6 + n][0:E, :]).then_inc(cwT_ready, 1)
            dve.wait_ge(x2_ready, B)
            dve.wait_ge(cw_ready, 1)
            for n in range(2):
                dve.wait_ge(b2_mm, n + 1)
                v.tensor_tensor(acc[:, 4 * n:4 * n + 4, :], x2[:, 4 * n:4 * n + 4, :],
                                bank[4 + n][:].rearrange("p (b d) -> p b d", b=4), ALU.add).then_inc(acc_done, 4)
            for e in range(E):
                for b in range(B):
                    if b % 4 == 0:
                        dve.wait_ge(down_mm, 2 * e + b // 4 + 1)
                    dve.wait_ge(acc_done, 8 * (e + 1) - 7 + b if e else 8)
                    v.scalar_tensor_tensor(out=acc[:, b, :], in0=bank[4 + (2 * e + b // 4) % 4][:, D * (b % 4):D * (b % 4) + D],
                                           scalar=stat("cw", E * b + e, 1), in1=acc[:, b, :],
                                           op0=ALU.mult, op1=ALU.add).then_inc(acc_done, 1)
            dve.wait_ge(acc_done, 8 * (E + 1))
            layer_norm(2, acc, fin, fin_ready)


INS = ["x", "ctx_1024", "L0_attn_w_qkv", "L0_attn_w_conv", "L0_attn_w_fc", "L0_attn_b_fc", "L0_ffn_gate_w",
       "L0_ffn_w1", "L0_ffn_b1", "L0_ffn_w2", "L0_ffn_b2"]


def kernel(**inputs):
    import numpy as np
    import concourse.bacc as bacc
    from concourse.bass_utils import run_bass_kernel_spmd

    nc = bacc.Bacc("TRN2", target_bir_lowering=False, num_devices=1)
    arrays, args = {}, []
    for name in INS:
        a = np.ascontiguousarray(inputs[name])
        arrays["in_" + name] = a
        args.append(nc.dram_tensor("in_" + name, a.shape, mybir.dt.from_np(a.dtype), kind="ExternalInput").ap())
    args.append(nc.dram_tensor("out_x", (B, N, D), F32, kind="ExternalOutput").ap())
    program(nc, *args)
    r = run_bass_kernel_spmd(nc, [arrays], core_ids=[0])
    return r.results[0]["out_x"]
```

```python
from contextlib import ExitStack

import concourse.bass as bass
from concourse import mybir

F32 = mybir.dt.float32
U32 = mybir.dt.uint32
ALU = mybir.AluOpType
ACT = mybir.ActivationFunctionType
AX_X = mybir.AxisListType.X

P = 128
B, N, D = 8, 128, 128
H, DH = 16, 64
M = 32
L = N // M
ITERS = 6
K = 13
S = 77
E, F = 8, 512
FK = F // P
PAIRS = H // 2
HG = H // 4
GROUPS = B * HG
CH = 4
GC = GROUPS // CH
NB = B * N // P + E - 1
EPS = 1e-5
BANK = 512


def cubic_factors():
    r = 4.0
    for _ in range(60):
        r -= (((r - 7) * r + 15) * r - 13) / ((3 * r - 14) * r + 15)
    return r, r - 7, 13 / r


ROOT, QB, QA = cubic_factors()


def program(nc, x, ctx_in, w_qkv, w_conv, w_fc, b_fc, gate_w, w1, b1, w2, b2, out):
    ctx = ExitStack()
    with ctx:
        def sb(name, shape, dtype=F32):
            return ctx.enter_context(nc.sbuf_tensor(name, shape, dtype))

        def sem(name):
            return ctx.enter_context(nc.semaphore(name))

        bank = [ctx.enter_context(nc.psum_tensor(f"bank{i}", [P, BANK], F32)) for i in range(8)]

        ident = sb("ident", [P, P])
        eye_a = sb("eye_a", [P, M])
        ones = sb("ones", [1, P])
        x_sb = sb("x_sb", [P, B, D])
        xT = sb("xT", [P, B * N])
        xl = sb("xl", [P, B * M])
        wqkv = sb("wqkv", [P, 3 * H * DH])
        WT = sb("WT", [P, 3, PAIRS, D])
        wfc = sb("wfc", [P, PAIRS, D])
        NV = sb("NV", [P, H, D])
        qkl = sb("qkl", [P, PAIRS, 2, B * M])
        GG = sb("GG", [P, B, 2, H, M])
        A1 = sb("A1", [P, B, H, M])
        E3 = sb("E3", [P, B, HG, N])
        E3T = sb("E3T", [P, 2, BANK])
        YT = sb("YT", [P, 2, BANK])
        A2 = sb("A2", [P, GROUPS, M])
        A2T = sb("A2T", [P, GROUPS, M])
        V = sb("V", [P, GROUPS, 2, M])
        MM = sb("MM", [P, GROUPS, 2, M])
        GB = sb("GB", [P, GROUPS, M])
        Tt = sb("Tt", [P, H, N])
        taps = sb("taps", [H, K])
        tapr = sb("tapr", [H, 2 * P - 1])
        ctxn = sb("ctxn", [S, B, D])
        ctxT = sb("ctxT", [P, B, S])
        bfc = sb("bfc", [P, D])
        xb = sb("xb", [P, B, D])
        gw = sb("gw", [P, E])
        w1s = sb("w1s", [P, E, F])
        b1n = sb("b1n", [E * FK, P])
        b1T = sb("b1T", [P, E * FK])
        b2s = sb("b2s", [E, D])
        st = sb("st", [P, 1152])
        prio = sb("prio", [P, E])
        before = sb("before", [P, P])
        ones_pp = sb("ones_pp", [P, P])
        full_at = sb("full_at", [P, 8])
        upto = sb("upto", [P, E, E])
        block_no = sb("block_no", [1, NB])
        slot_u = sb("slot_u", [P, B], U32)
        expert_u = sb("expert_u", [1, NB], U32)

        gg_flat = GG[:].rearrange("p b w h m -> p (b w h m)")
        b1T3 = b1T[:].rearrange("p (e k) -> p e k", e=E)
        CC = gg_flat[:, 0:4096].rearrange("p (b h m) -> p b h m", b=B, h=H)
        U = gg_flat[:, 4096:8192].rearrange("p (b g d) -> p b g d", b=B, g=HG)
        CT = A1[:].rearrange("p b h m -> p (b h m)").rearrange("p (b g n) -> p b g n", b=B, g=HG)
        xTr = GB[:].rearrange("p g m -> p (g m)").rearrange("p (b n) -> p b n", b=B)
        R = E3
        v_flat = V[:].rearrange("p g w m -> p (g w m)")
        gx = v_flat[0:S, 0:1024].rearrange("p (b n) -> p b n", b=B)
        cwT = v_flat[0:E, 1024:2048]
        w2s = E3[:].rearrange("p b g n -> p (b g n)").rearrange("p (e k d) -> p e k d", e=E, k=FK)
        y = wqkv[:, 0:1024].rearrange("p (b d) -> p b d", b=B)
        x1 = wqkv[:, 1024:2048].rearrange("p (b d) -> p b d", b=B)
        xTn = wqkv[:, 2048:3072]
        x2 = xb
        acc = MM[:].rearrange("p g w m -> p (g w m)")[:, 0:1024].rearrange("p (b d) -> p b d", b=B)
        fin = MM[:].rearrange("p g w m -> p (g w m)")[:, 1024:2048].rearrange("p (b d) -> p b d", b=B)
        qk_flat = qkl[:].rearrange("p a w c -> p (a w c)")
        xs = WT[:].rearrange("p w a d -> p (w a d)")[:, 0:NB * D].rearrange("p (j d) -> p j d", j=NB)
        xsT = qk_flat[:, 0:NB * P].rearrange("p (j t) -> p j t", j=NB)
        ys = qk_flat[:, NB * P:2 * NB * P].rearrange("p (j d) -> p j d", j=NB)
        hn = gg_flat[:, 0:3 * F].rearrange("p (s f) -> p s f", s=3)
        hT = gg_flat[:, 2048:2048 + 3 * F].rearrange("p (s c) -> p s c", s=3)
        yg = gg_flat[:, 4096:5120].rearrange("p (b d) -> p b d", b=B)

        Pd = qkl[:].rearrange("p a w c -> p (a w c)").rearrange("p (g c) -> p g c", g=GROUPS)
        Qd = WT[:].rearrange("p w a d -> p (w a d)").rearrange("p (s g c) -> p s g c", s=3, g=GC)

        in_x, in_wq, in_wk, in_wv = sem("in_x"), sem("in_wq"), sem("in_wk"), sem("in_wv")
        in_wfc, in_ctx, in_taps, in_bfc = sem("in_wfc"), sem("in_ctx"), sem("in_taps"), sem("in_bfc")
        in_ffn, in_b1, taps_out, in_T = sem("in_ffn"), sem("in_b1"), sem("taps_out"), sem("in_T")
        out_done = sem("out_done")
        zero_done, ident_ready, const_ready = sem("zero_done"), sem("ident_ready"), sem("const_ready")
        taps_zero, taps_rev, taps_ready, xb_ready = (sem("taps_zero"), sem("taps_rev"), sem("taps_ready"),
                                                     sem("xb_ready"))
        ve, ac = sem("vector_step"), sem("scalar_step")
        xT_mm, xT_ready, xl_ready = sem("xT_mm"), sem("xT_ready"), sem("xl_ready")
        xTr_ready = sem("xTr_ready")
        qkl_mm, qkl_even, qkl_odd = sem("qkl_mm"), sem("qkl_even"), sem("qkl_odd")
        sim2_mm, sim2_shift, sim2_exp = sem("sim2_mm"), sem("sim2_shift"), sem("sim2_exp")
        A2_ready, A2T_ready = sem("A2_ready"), sem("A2T_ready")
        WT_mm, WT_ready = sem("WT_mm"), sem("WT_ready")
        GG_mm, GG_even, GG_odd = sem("GG_mm"), sem("GG_even"), sem("GG_odd")
        peak_ready, peak_mm, cinv_ready, c_mm, c_ready = (sem("peak_ready"), sem("peak_mm"), sem("cinv_ready"),
                                                          sem("c_mm"), sem("c_ready"))
        P0_mm, P0_ready, W0_ready = sem("P0_mm"), sem("P0_ready"), sem("W0_ready")
        ctxT_mm, ctxT_ready, b1T_mm, b1T_ready = sem("ctxT_mm"), sem("ctxT_ready"), sem("b1T_mm"), sem("b1T_ready")
        NV_mm, NV_ready = sem("NV_mm"), sem("NV_ready")
        sim1_mm, sim1_shift, exp1_done, rsum1, A1_ready = (sem("sim1_mm"), sem("sim1_shift"), sem("exp1_done"),
                                                           sem("rsum1"), sem("A1_ready"))
        sim3_mm, max3_ready, exp3_done, rsum3, attn3_ready = (sem("sim3_mm"), sem("max3_ready"), sem("exp3_done"),
                                                              sem("rsum3"), sem("attn3_ready"))
        E3T_mm, E3T_ready, YT_mm, YT_ready = sem("E3T_mm"), sem("E3T_ready"), sem("YT_mm"), sem("YT_ready")
        R_mm, R_ready = sem("R_mm"), sem("R_ready")
        C_mm, C_even, C_odd = sem("C_mm"), sem("C_even"), sem("C_odd")
        CT_mm, CT_even, CT_odd = sem("CT_mm"), sem("CT_even"), sem("CT_odd")
        PV_mm, MQ_ready, QM_mm, V_ready = sem("PV_mm"), sem("MQ_ready"), sem("QM_mm"), sem("V_ready")
        U_mm, U_even, U_odd = sem("U_mm"), sem("U_even"), sem("U_odd")
        Pd_zero, Qd_zero = sem("Pd_zero"), sem("Qd_zero")
        attn_mm, var_ready, std_ready, x1_ready = sem("attn_mm"), sem("var_ready"), sem("std_ready"), sem("x1_ready")
        x1T_mm, x1T_ready, cs_mm, gx_ready, xa_mm = (sem("x1T_mm"), sem("x1T_ready"), sem("cs_mm"), sem("gx_ready"),
                                                     sem("xa_mm"))
        x2_ready, x2T_mm, x2T_ready = sem("x2_ready"), sem("x2T_mm"), sem("x2T_ready")
        gate_mm, gate_shift, gate_exp, cw_ready = sem("gate_mm"), sem("gate_shift"), sem("gate_exp"), sem("cw_ready")
        cwT_mm, cwT_ready, b2_mm = sem("cwT_mm"), sem("cwT_ready"), sem("b2_mm")
        route_const, sel_ready, nsel_ready, rank_mm = (sem("route_const"), sem("sel_ready"), sem("nsel_ready"),
                                                       sem("rank_mm"))
        slot_ready, expert_ready = sem("slot_ready"), sem("expert_ready")
        xs_zero, xs_cleared, xs_sent = sem("xs_zero"), sem("xs_cleared"), sem("xs_sent")
        xs_loaded = [sem(f"xs_loaded{n}") for n in range(3)]
        xsT_mm, xsT_ready = sem("xsT_mm"), sem("xsT_ready")
        up_mm, hn_ready, hn_mm, h_ready, down_mm, ys_ready = (sem("up_mm"), sem("hn_ready"), sem("hn_mm"),
                                                              sem("h_ready"), sem("down_mm"), sem("ys_ready"))
        yg_loaded = [sem(f"yg_loaded{b}") for b in range(B)]
        ys_sent, base_ready, acc_ready, fin_ready = (sem("ys_sent"), sem("base_ready"),
                                                                sem("acc_ready"), sem("fin_ready"))

        padded = nc.dram_tensor("padded_taps", (H, 2 * P - 1), F32)
        xs_dram = nc.dram_tensor("sorted_tokens", (NB * P, D), F32)
        ys_dram = nc.dram_tensor("sorted_outputs", (NB * P, D), F32)
        toeplitz = bass.AP(padded, 0, [[1, P], [2 * P - 1, H], [1, N]])

        cols = {}
        at = 0
        for name, n in (("mx2", GROUPS), ("rs2", GROUPS), ("cs", GROUPS), ("rows", GROUPS), ("peak", 2), ("pk", 2),
                        ("prod", 1), ("cinv", 1), ("c", 1), ("mx1", B * H), ("rs1", B * H), ("nm3", B * HG),
                        ("s3", B * HG), ("r3", B * HG), ("bn", 6 * B), ("mv", 2 * B), ("sd", B), ("rstd", B),
                        ("gmx", B), ("grs", B), ("gp", B * E), ("gpm", B), ("gsm", B), ("cw", B * E),
                        ("gm", B * E), ("nsel", E), ("cmp", E * 8), ("nb", E), ("cum", E), ("start", E),
                        ("slots", B * E), ("slot", B), ("bcmp", NB * E), ("bexp", NB)):
            cols[name] = (at, n)
            at += n

        def stat(name, lo=0, n=None):
            a, k = cols[name]
            return st[:, a + lo:a + lo + (k if n is None else n)]

        steps = ITERS * CH

        def v_count(k):
            return 5 * (k + 1) if k < steps - CH else 5 * (steps - CH) + 4 * (k + 1 - (steps - CH))

        def slot_rows(t):
            return t.ap().rearrange("(j p) d -> p j d", p=P)

        def quad(q):
            return slice(M * q, M * (q + 1))

        block = ctx.enter_context(nc.Block())

        @block.sync
        def _(sp):
            sp.dma_start(x_sb[:], x.rearrange("b n d -> n b d")).then_inc(in_x, 16)
            sp.dma_start(wqkv[:, 0:1024], w_qkv[:, 0:1024]).then_inc(in_wq, 16)
            sp.dma_start(wqkv[:, 1024:2048], w_qkv[:, 1024:2048]).then_inc(in_wk, 16)
            sp.dma_start(wqkv[:, 2048:3072], w_qkv[:, 2048:3072]).then_inc(in_wv, 16)
            sp.dma_start(taps[:], w_conv.rearrange("h a k b -> h (a k b)")).then_inc(in_taps, 16)
            sp.dma_start(wfc[:], w_fc.rearrange("(p c) d -> c p d", c=P)).then_inc(in_wfc, 16)
            sp.dma_start(ctxn[:], ctx_in.rearrange("b s d -> s b d")).then_inc(in_ctx, 16)
            sp.dma_start(bfc[:], b_fc.rearrange("(a d) -> a d", a=1).broadcast_to([P, D])).then_inc(in_bfc, 16)
            sp.dma_start(b1n[:], b1.rearrange("e (k p) -> (e k) p", k=FK)).then_inc(in_b1, 16)
            sp.wait_ge(taps_ready, 1)
            sp.dma_start(padded.ap(), tapr[:]).then_inc(taps_out, 16)
            sp.wait_ge(taps_out, 16)
            sp.dma_start(Tt[:], toeplitz).then_inc(in_T, 16)
            sp.dma_start(gw[:], gate_w).then_inc(in_ffn, 16)
            sp.dma_start(b2s[:], b2).then_inc(in_ffn, 16)
            sp.dma_start(w1s[:], w1.rearrange("e d f -> d e f")).then_inc(in_ffn, 16)
            sp.wait_ge(U_mm, B)
            sp.dma_start(w2s, w2.rearrange("e (k p) d -> p e k d", k=FK)).then_inc(in_ffn, 16)
            sp.wait_ge(xs_zero, 1)
            sp.dma_start(slot_rows(xs_dram), xs).then_inc(xs_cleared, 16)
            sp.wait_ge(xs_sent, 16 * B)
            for n in range(3):
                js = slice(5 * n, 5 * n + 5)
                sp.dma_start(xs[:, js, :], slot_rows(xs_dram)[:, js, :]).then_inc(xs_loaded[n], 16)
            for j in range(NB):
                sp.wait_ge(ys_ready, j + 1)
                sp.dma_start(slot_rows(ys_dram)[:, j, :], ys[:, j, :]).then_inc(ys_sent, 16)
            sp.wait_ge(fin_ready, B)
            sp.dma_start(out.rearrange("b n d -> n b d"), fin).then_inc(out_done, 16)
            sp.wait_ge(out_done, 16)

        @block.gpsimd
        def _(pool):
            nc.gpsimd.memset(ident[:], 0.0).then_inc(zero_done, 1)
            pool.wait_ge(zero_done, 1)
            nc.gpsimd.affine_select(out=ident[:], in_=ident[:], compare_op=ALU.not_equal, fill=1.0, base=0,
                                    pattern=[[-1, P]], channel_multiplier=1).then_inc(ident_ready, 1)
            nc.gpsimd.memset(tapr[:], 0.0).then_inc(taps_zero, 1)
            nc.gpsimd.memset(ones[:], 1.0).then_inc(const_ready, 1)
            for e in range(E):
                nc.gpsimd.memset(prio[:, e:e + 1], float(E - e)).then_inc(const_ready, 1)
            nc.gpsimd.memset(before[:], 1.0).then_inc(route_const, 1)
            nc.gpsimd.memset(ones_pp[:], 1.0).then_inc(route_const, 1)
            nc.gpsimd.memset(upto[:], 0.0).then_inc(route_const, 1)
            for k in range(8):
                nc.gpsimd.memset(full_at[:, k:k + 1], float(P * k)).then_inc(route_const, 1)
            for j in range(NB):
                nc.gpsimd.memset(block_no[:, j:j + 1], float(j)).then_inc(route_const, 1)
            pool.wait_ge(route_const, 3 + 8 + NB)
            nc.gpsimd.affine_select(out=before[:], in_=before[:], compare_op=ALU.is_gt, fill=0.0, base=0,
                                    pattern=[[1, P]], channel_multiplier=-1).then_inc(route_const, 1)
            for e in range(E):
                nc.gpsimd.memset(upto[:, e, 0:e + 1], 1.0).then_inc(route_const, 1)
            pool.wait_ge(taps_zero, 1)
            pool.wait_ge(in_taps, 16)
            first = P - 1 - K // 2
            nc.gpsimd.tensor_copy(tapr[:, first:first + K], taps[:, ::-1]).then_inc(taps_rev, 1)
            pool.wait_ge(taps_rev, 1)
            nc.gpsimd.tensor_scalar(tapr[:, P - 1:P], tapr[:, P - 1:P], 1.0, None, ALU.add).then_inc(taps_ready, 1)
            pool.wait_ge(ident_ready, 1)
            for q in range(4):
                eye = ident[quad(q), quad(q)]
                nc.gpsimd.tensor_scalar(eye_a[quad(q), :], eye, QA, None, ALU.mult).then_inc(const_ready, 1)
            pool.wait_ge(const_ready, 1 + E + 4)
            pool.wait_ge(xT_ready, 2)
            nc.gpsimd.tensor_copy(xTr, xT[:].rearrange("p (b n) -> p b n", b=B)[:, :, ::-1]).then_inc(xTr_ready, 1)
            pool.wait_ge(in_bfc, 16)
            nc.gpsimd.tensor_tensor(xb[:], x_sb[:], bfc[:].unsqueeze(1).broadcast_to([P, B, D]), ALU.add
                                    ).then_inc(xb_ready, 1)
            pool.wait_ge(GG_mm, H)
            nc.gpsimd.memset(Pd, 0.0).then_inc(Pd_zero, 1)
            pool.wait_ge(c_ready, 1)
            for n in range(2):
                nc.gpsimd.tensor_scalar(V[:, 16 * n:16 * n + 16, 1, :], A2[:, 16 * n:16 * n + 16], stat("c"), None,
                                        ALU.mult).then_inc(W0_ready, 1)
            for b in range(B):
                pool.wait_ge(rsum3, b + 1)
                nc.gpsimd.tensor_tensor(E3[:, b], E3[:, b], stat("r3", HG * b, HG).unsqueeze(2)
                                        .broadcast_to([P, HG, N]), ALU.mult).then_inc(attn3_ready, 1)
                pool.wait_ge(rsum1, b + 1)
                nc.gpsimd.tensor_tensor(A1[:, b], A1[:, b], stat("rs1", H * b, H).unsqueeze(2)
                                        .broadcast_to([P, H, M]), ALU.mult).then_inc(A1_ready, 1)
            pool.wait_ge(NV_mm, 2)
            nc.gpsimd.memset(Qd, 0.0).then_inc(Qd_zero, 1)
            pool.wait_ge(QM_mm, steps)
            nc.gpsimd.memset(xs, 0.0).then_inc(xs_zero, 1)
            pool.wait_ge(x2_ready, B)
            pool.wait_ge(xs_cleared, 16)
            pool.wait_ge(slot_ready, 1)
            for b in range(B):
                nc.gpsimd.indirect_dma_start(out=xs_dram.ap(), out_offset=bass.IndirectOffsetOnAxis(slot_u[:, b:b + 1], 0),
                                             in_=x2[:, b, :], in_offset=None).then_inc(xs_sent, 16)
            pool.wait_ge(ys_sent, 16 * NB)
            for b in range(B):
                nc.gpsimd.indirect_dma_start(out=yg[:, b, :], out_offset=None, in_=ys_dram.ap(),
                                             in_offset=bass.IndirectOffsetOnAxis(slot_u[:, b:b + 1], 0)
                                             ).then_inc(yg_loaded[b], 16)

        @block.tensor
        def _(pe):
            mm, tr = nc.tensor.matmul, nc.tensor.transpose
            pe.wait_ge(ident_ready, 1)
            pe.wait_ge(in_x, 16)
            for b in range(B):
                i = tr(bank[b // 4][:, P * (b % 4):P * (b % 4 + 1)], x_sb[:, b, :], ident[:])
                if b % 4 == 3:
                    i.then_inc(xT_mm, 1)
            pe.wait_ge(xl_ready, 1)
            pe.wait_ge(in_wq, 16)
            pe.wait_ge(in_wk, 16)
            for p in range(PAIRS):
                for w in range(2):
                    i = mm(bank[(2 + p) % 8][:, 256 * w:256 * w + 256], wqkv[:, 1024 * w + P * p:1024 * w + P * p + P],
                           xl[:], start=True, stop=True)
                i.then_inc(qkl_mm, 1)
            pe.wait_ge(qkl_even, PAIRS // 2)
            pe.wait_ge(qkl_odd, PAIRS // 2)
            for b in range(B):
                for h in range(H):
                    k = slice(DH * (h % 2), DH * (h % 2) + DH)
                    c = ((b % 4) * HG + h // 4) * M
                    i = mm(bank[2 + b // 4][quad(h % 4), c:c + M], qkl[k, h // 2, 0, M * b:M * b + M],
                           qkl[k, h // 2, 1, M * b:M * b + M], start=True, stop=True)
                if b % 4 == 3:
                    i.then_inc(sim2_mm, 1)
            for n in range(3 * PAIRS):
                if n == 2 * PAIRS:
                    pe.wait_ge(in_wv, 16)
                i = tr(bank[(4 + n // 4) % 8][:, P * (n % 4):P * (n % 4) + P], wqkv[:, P * n:P * n + P], ident[:])
                if n % 4 == 3:
                    i.then_inc(WT_mm, 1)
            pe.wait_ge(WT_ready, 6)
            for h in range(H):
                if h < 2:
                    pe.wait_ge(sim2_shift, h + 1)
                if h >= 8:
                    pe.wait_ge(GG_even if h % 2 == 0 else GG_odd, (h - 8) // 2 + 1)
                k = slice(DH * (h % 2), DH * (h % 2) + DH)
                mm(bank[(2 + h) % 8][:, 0:256], WT[k, 0, h // 2, :], qkl[k, h // 2, 1, :], start=True, stop=True)
                mm(bank[(2 + h) % 8][:, 256:512], WT[k, 1, h // 2, :], qkl[k, h // 2, 0, :],
                   start=True, stop=True).then_inc(GG_mm, 1)
            pe.wait_ge(peak_ready, 1)
            pe.wait_ge(GG_even, 7)
            for w in range(2):
                i = tr(bank[6][0:1, P * w:P * w + P], stat("peak", w, 1), ident[:])
            i.then_inc(peak_mm, 1)

            def head_values(n, first, second):
                for p in range(4 * n, 4 * n + 4):
                    for w in range(2):
                        k = slice(DH * w, DH * w + DH)
                        c = P * (p % 4)
                        i = mm(bank[second if w else first][:, c:c + P], WT[k, 2, p, :], wfc[k, p, :],
                               start=True, stop=True)
                i.then_inc(NV_mm, 1)

            def context_transposed(n):
                for b in range(4 * n, 4 * n + 4):
                    i = tr(bank[7][:, S * (b % 4):S * (b % 4) + S], ctxn[:, b, :], ident[0:S, 0:S])
                i.then_inc(ctxT_mm, 1)

            def squares(n):
                for g in range(16 * n, 16 * n + 16):
                    for q in range(4):
                        t = A2T[quad(q), g, :]
                        i = mm(bank[3 + n][quad(q), M * (g % 16):M * (g % 16) + M], t, t, start=True, stop=True)
                i.then_inc(P0_mm, 1)

            pe.wait_ge(in_wfc, 16)
            pe.wait_ge(GG_odd, 7)
            head_values(0, 4, 7)
            pe.wait_ge(const_ready, 1)
            pe.wait_ge(cinv_ready, 1)
            mm(bank[6][:, 256:257], ones[:], stat("cinv")[0:1, :], start=True, stop=True).then_inc(c_mm, 1)
            pe.wait_ge(A2T_ready, 1)
            pe.wait_ge(GG_even, 8)
            pe.wait_ge(GG_odd, 8)
            pe.wait_ge(xTr_ready, 1)
            for s in range(B + 5):
                if s < B:
                    if s >= 2:
                        pe.wait_ge(sim1_shift, s - 1)
                    mm(bank[1 + s % 2][:], xTr[:, s, :], GG[:, s, 0].rearrange("p h m -> p (h m)"),
                       start=True, stop=True).then_inc(sim1_mm, 1)
                    if s == 1:
                        pe.wait_ge(c_ready, 1)
                    if s >= 2:
                        pe.wait_ge(exp3_done, HG * (s - 1))
                    for g in range(HG):
                        i = mm(bank[5 + s % 2][:, N * g:N * g + N], GG[:, s, 1, 4 * g:4 * g + 4].rearrange("p h m -> p (h m)"),
                               xT[:, N * s:N * s + N], start=True, stop=True)
                    i.then_inc(sim3_mm, 1)
                if s == 0:
                    pe.wait_ge(NV_ready, 1)
                    pe.wait_ge(in_ctx, 16)
                    context_transposed(0)
                    squares(0)
                if s == 1:
                    pe.wait_ge(ctxT_ready, 1)
                    context_transposed(1)
                    pe.wait_ge(in_b1, 16)
                    tr(bank[0][:, 0:E * FK], b1n[:], ident[0:E * FK, 0:E * FK]).then_inc(b1T_mm, 1)
                    squares(1)
                if s == 2:
                    pe.wait_ge(b1T_ready, 1)
                    pe.wait_ge(ctxT_ready, 2)
                    head_values(1, 0, 7)
                if s == 3:
                    pe.wait_ge(NV_ready, 2)
                if 3 <= s < B + 3:
                    b = s - 3
                    pe.wait_ge(attn3_ready, b + 1)
                    if b >= 1:
                        pe.wait_ge(E3T_ready, b)
                    for g in range(HG):
                        i = tr(bank[7][:, P * g:P * g + P], E3[:, b, g, :], ident[:])
                    i.then_inc(E3T_mm, 1)
                if 4 <= s < B + 4:
                    b = s - 4
                    pe.wait_ge(E3T_ready, b + 1)
                    if b >= 1:
                        pe.wait_ge(YT_ready, b)
                    mm(bank[0][:], x_sb[:, b, :], E3T[:, b % 2, :], start=True, stop=True).then_inc(YT_mm, 1)
                if s >= 5:
                    b = s - 5
                    pe.wait_ge(YT_ready, b + 1)
                    if b < 2:
                        pe.wait_ge(P0_ready, 5 * (b + 1))
                    if b >= 2:
                        pe.wait_ge(R_ready, b - 1)
                    for h in range(H):
                        i = mm(bank[3 + b % 2][quad(h % 4), P * (h // 4):P * (h // 4) + P],
                               YT[:, b % 2, M * h:M * h + M], NV[:, h, :], start=True, stop=True)
                    i.then_inc(R_mm, 1)
            def convolution(first):
                for p in range(first, first + 4):
                    if p >= 4:
                        pe.wait_ge(C_even if p % 2 == 0 else C_odd, (p - 4) // 2 + 1)
                    for w in range(2):
                        i = mm(bank[4 + p % 4][:, 256 * w:256 * w + 256], Tt[:, 2 * p + w, :], A1[:, :, 2 * p + w, :],
                               start=True, stop=True)
                    i.then_inc(C_mm, 1)

            pe.wait_ge(W0_ready, 2)
            pe.wait_ge(YT_ready, B)
            pe.wait_ge(sim1_shift, B)
            pe.wait_ge(exp3_done, HG * B)
            pe.wait_ge(R_ready, B - 1)
            pe.wait_ge(in_T, 16)
            pe.wait_ge(A1_ready, B)
            for k in range(steps + 2):
                if k == steps:
                    pe.wait_ge(R_ready, B)
                    convolution(0)
                if k == steps + 1:
                    convolution(4)
                if k < steps:
                    c = k % CH
                    if k >= CH:
                        pe.wait_ge(V_ready, 5 * (k - CH + 1))
                    if k >= 2:
                        pe.wait_ge(MQ_ready, 5 * (k - 1))
                    for g in range(GC):
                        i = mm(bank[c % 2][:, 64 * g:64 * g + 64], Pd[:, GC * c + g, :], V[:, GC * c + g],
                               start=True, stop=True)
                    i.then_inc(PV_mm, 1)
                if k >= 2:
                    j = k - 2
                    c, last = j % CH, j >= steps - CH
                    pe.wait_ge(MQ_ready, 5 * (j + 1))
                    if j >= 2:
                        pe.wait_ge(V_ready, v_count(j - 2))
                    for g in range(GC):
                        i = mm(bank[2 + c % 2][:, 64 * g + M * last:64 * g + 64], Qd[:, j % 3, g, :],
                               MM[:, GC * c + g, 1 if last else 0:2, :], start=True, stop=True)
                    i.then_inc(QM_mm, 1)
            pe.wait_ge(C_even, 4)
            pe.wait_ge(C_odd, 4)
            for b in range(B):
                if b >= 4:
                    pe.wait_ge(CT_even if b % 2 == 0 else CT_odd, (b - 4) // 2 + 1)
                for g in range(HG):
                    i = tr(bank[4 + b % 4][:, N * g:N * g + N], CC[:, b, 4 * g:4 * g + 4].rearrange("p h m -> p (h m)"),
                           ident[:])
                i.then_inc(CT_mm, 1)
            pe.wait_ge(V_ready, v_count(steps - 1))
            for b in range(B):
                if b >= 4:
                    pe.wait_ge(U_even if b % 2 == 0 else U_odd, (b - 4) // 2 + 1)
                for g in range(HG):
                    i = mm(bank[b % 4][:, D * g:D * g + D], Pd[:, HG * b + g, :], R[:, b, g, :],
                           start=True, stop=True)
                i.then_inc(U_mm, 1)
            pe.wait_ge(CT_even, 4)
            pe.wait_ge(CT_odd, 4)
            for b in range(B):
                pe.wait_ge(U_even if b % 2 == 0 else U_odd, b // 2 + 1)
                for g in range(HG):
                    i = mm(bank[4 + b // 4][:, D * (b % 4):D * (b % 4) + D], CT[:, b, g, :], U[:, b, g, :],
                           start=(g == 0), stop=(g == HG - 1))
                if b % 4 == 3:
                    i.then_inc(attn_mm, 1)
            for b in range(B):
                pe.wait_ge(x1_ready, b + 1)
                i = tr(bank[b // 4][:, N * (b % 4):N * (b % 4) + N], x1[:, b, :], ident[:])
                if b % 4 == 3:
                    i.then_inc(x1T_mm, 1)
            for b in range(B):
                pe.wait_ge(x1T_ready, b // 4 + 1)
                i = mm(bank[2 + b // 4][0:S, N * (b % 4):N * (b % 4) + N], ctxT[:, b, :], xTn[:, N * b:N * b + N],
                       start=True, stop=True)
                if b % 4 == 3:
                    i.then_inc(cs_mm, 1)
            for b in range(B):
                pe.wait_ge(gx_ready, b // 4 + 1)
                i = mm(bank[4 + b // 4][:, D * (b % 4):D * (b % 4) + D], gx[:, b, :], ctxn[:, b, :],
                       start=True, stop=True)
                if b % 4 == 3:
                    i.then_inc(xa_mm, 1)
            for b in range(B):
                pe.wait_ge(x2_ready, b + 1)
                i = tr(bank[b // 4][:, N * (b % 4):N * (b % 4) + N], x2[:, b, :], ident[:])
                if b % 4 == 3:
                    i.then_inc(x2T_mm, 1)
            pe.wait_ge(in_ffn, 64)
            for b in range(B):
                pe.wait_ge(x2T_ready, b // 4 + 1)
                i = mm(bank[2][:, E * b:E * b + E], xTn[:, N * b:N * b + N], gw[:], start=True, stop=True)
            i.then_inc(gate_mm, 1)

            pe.wait_ge(route_const, 3 + 8 + NB + 1 + E)
            pe.wait_ge(sel_ready, 1)
            for b in range(B - 1):
                later = stat("gm", E * b, E).unsqueeze(1).broadcast_to([P, B - 1 - b, E])
                mm(bank[3][:, E * (b + 1):B * E], ones_pp[:], later, start=(b == 0), stop=False,
                   skip_group_check=True)
            mm(bank[3][:, 0:B * E], before[:], stat("gm"), start=False, stop=True, skip_group_check=True)
            pe.wait_ge(nsel_ready, 1)
            mm(bank[2][:, B * E:B * E + E], ones_pp[:], stat("nsel"), start=True, stop=True).then_inc(rank_mm, 1)
            pe.wait_ge(cw_ready, 1)
            for b in range(B):
                i = tr(bank[6 + b // 4][0:E, N * (b % 4):N * (b % 4) + N], stat("cw", E * b, E), ident[:])
                if b % 4 == 3:
                    i.then_inc(cwT_mm, 1)
            for b in range(B):
                pe.wait_ge(cwT_ready, b // 4 + 1)
                i = mm(bank[4 + b // 4][:, D * (b % 4):D * (b % 4) + D], cwT[:, N * b:N * b + N], b2s[:],
                       start=True, stop=True)
                if b % 4 == 3:
                    i.then_inc(b2_mm, 1)
            pe.wait_ge(expert_ready, 1)
            experts = [pe.value_load(expert_u[0:1, j:j + 1], min_val=0, max_val=E - 1) for j in range(NB)]
            pe.wait_ge(slot_ready, 1)
            for j in range(NB):
                pe.wait_ge(xs_loaded[j // 5], 16)
                i = tr(bank[j // 4][:, P * (j % 4):P * (j % 4) + P], xs[:, j, :], ident[:])
                if j % 4 == 3 or j == NB - 1:
                    i.then_inc(xsT_mm, 1)
            pe.wait_ge(base_ready, 2)
            for s in range(NB + 2):
                if s < NB:
                    if s == 0:
                        pe.wait_ge(xsT_ready, 4)
                    if s >= 2:
                        pe.wait_ge(hn_ready, s - 1)
                    mm(bank[s % 2][:], xsT[:, s, :], w1s[:, experts[s], :], start=True, stop=True).then_inc(up_mm, 1)
                if 1 <= s < NB + 1:
                    j = s - 1
                    pe.wait_ge(hn_ready, j + 1)
                    if j >= 2:
                        pe.wait_ge(h_ready, FK * (j - 1))
                    for k in range(FK):
                        i = tr(bank[2 + j % 2][:, P * k:P * k + P], hn[:, j % 3, P * k:P * k + P], ident[:])
                    i.then_inc(hn_mm, 1)
                if s >= 2:
                    j = s - 2
                    pe.wait_ge(h_ready, FK * (j + 1))
                    if j >= 2:
                        pe.wait_ge(ys_ready, j - 1)
                    for k in range(FK):
                        i = mm(bank[4 + j % 2][:, 0:D], hT[:, j % 3, P * k:P * k + P], w2s[:, experts[j], k, :],
                               start=(k == 0), stop=(k == FK - 1))
                    i.then_inc(down_mm, 1)

        @block.scalar
        def _(act):
            n_ac = 0
            for p in range(1, PAIRS, 2):
                act.wait_ge(qkl_mm, p + 1)
                nc.scalar.copy(qkl[:, p], bank[(2 + p) % 8][:].rearrange("p (w c) -> p w c", w=2)).then_inc(qkl_odd, 1)
            for n in range(6):
                act.wait_ge(WT_mm, n + 1)
                nc.scalar.copy(WT[:, n // 2, 4 * (n % 2):4 * (n % 2) + 4, :],
                               bank[(4 + n) % 8][:].rearrange("p (a d) -> p a d", a=4)).then_inc(WT_ready, 1)
                if n in (1, 3):
                    i = n // 2
                    act.wait_ge(sim2_shift, i + 1)
                    nc.scalar.activation(A2[:, 16 * i:16 * i + 16], A2[:, 16 * i:16 * i + 16], ACT.Exp,
                                         scale=DH ** -0.5 / L / L).then_inc(sim2_exp, 1)
            for h in range(0, H, 2):
                act.wait_ge(GG_mm, h + 1)
                nc.scalar.copy(GG[:, :, :, h, :].rearrange("p b w m -> p w b m"),
                bank[(2 + h) % 8][:].rearrange("p (w b m) -> p w b m", w=2, b=B)).then_inc(GG_even, 1)

            def head_values(n, first, second):
                act.wait_ge(NV_mm, n + 1)
                nc.scalar.copy(NV[:, 8 * n:8 * n + 8:2, :], bank[first][:].rearrange("p (a d) -> p a d", a=4)
                               ).then_inc(ac, 1)
                nc.scalar.copy(NV[:, 8 * n + 1:8 * n + 8:2, :], bank[second][:].rearrange("p (a d) -> p a d", a=4)
                               ).then_inc(NV_ready, 1)

            def context_transposed(n):
                act.wait_ge(ctxT_mm, n + 1)
                nc.scalar.copy(ctxT[:, 4 * n:4 * n + 4, :], bank[7][:, 0:4 * S].rearrange("p (a s) -> p a s", a=4)
                               ).then_inc(ctxT_ready, 1)

            def first_P(n, quads):
                act.wait_ge(P0_mm, n + 1)
                if 0 in quads:
                    act.wait_ge(c_ready, 1)
                    act.wait_ge(Pd_zero, 1)
                    nc.scalar.activation(V[:, 16 * n:16 * n + 16, 0, :],
                                         bank[3 + n][:].rearrange("p (g m) -> p g m", g=16),
                                         ACT.Copy, scale=stat("c")).then_inc(P0_ready, 1)
                for q in quads:
                    nc.scalar.activation(Pd[quad(q), 16 * n:16 * n + 16, quad(q)],
                                         bank[3 + n][quad(q), :].rearrange("p (g m) -> p g m", g=16),
                                         ACT.Copy, scale=stat("c")[quad(q), :]).then_inc(P0_ready, 1)

            head_values(0, 4, 7)
            for s in range(B + 5):
                if s < B:
                    act.wait_ge(sim1_shift, s + 1)
                    nc.scalar.activation(A1[:, s], A1[:, s], ACT.Exp, scale=DH ** -0.5 / L).then_inc(exp1_done, 1)
                    act.wait_ge(max3_ready, s + 1)
                    for g in range(HG):
                        nc.scalar.activation(E3[:, s, g, :], bank[5 + s % 2][:, N * g:N * g + N], ACT.Exp,
                                             bias=stat("nm3", HG * s + g, 1), scale=DH ** -0.5 / L,
                                             accum_out=stat("s3", HG * s + g, 1)).then_inc(exp3_done, 1)
                if s == 0:
                    context_transposed(0)
                if s == 1:
                    first_P(0, (0, 1))
                    context_transposed(1)
                    act.wait_ge(b1T_mm, 1)
                    nc.scalar.copy(b1T[:], bank[0][:, 0:E * FK]).then_inc(b1T_ready, 1)
                if s == 2:
                    head_values(1, 0, 7)
                    first_P(0, (2, 3))
                if s == 3:
                    first_P(1, (0, 1))
                if s == 4:
                    first_P(1, (2, 3))
                if 4 <= s < B + 4:
                    act.wait_ge(YT_mm, s - 3)
                    nc.scalar.copy(YT[:, (s - 4) % 2, :], bank[0][:]).then_inc(YT_ready, 1)
                if s >= 5:
                    b = s - 5
                    act.wait_ge(R_mm, b + 1)
                    nc.scalar.copy(R[:, b], bank[3 + b % 2][:].rearrange("p (g d) -> p g d", g=HG)).then_inc(R_ready, 1)
            for k in range(steps):
                c, last = k % CH, k >= steps - CH
                if k >= steps - 2:
                    for p in (1, 3) if k == steps - 2 else (5, 7):
                        act.wait_ge(C_mm, p + 1)
                        nc.scalar.copy(CC[:, :, 2 * p:2 * p + 2].rearrange("p b h m -> p h b m"),
                                       bank[4 + p % 4][:].rearrange("p (h b m) -> p h b m", h=2, b=B)
                                       ).then_inc(C_odd, 1)
                act.wait_ge(QM_mm, k + 1)
                if not last:
                    nc.scalar.mul(V[:, GC * c:GC * c + GC],
                                  bank[2 + c % 2][:].rearrange("p (g w m) -> p g w m", g=GC, w=2),
                                  0.25).then_inc(V_ready, 1)
                for q in range(4):
                    ps = bank[2 + c % 2][quad(q), :].rearrange("p (g w m) -> p g w m", g=GC, w=2)
                    nc.scalar.mul(Pd[quad(q), GC * c:GC * c + GC, quad(q)], ps[:, :, 1 if last else 0, :],
                                  0.25).then_inc(V_ready, 1)
            for b in range(1, B, 2):
                act.wait_ge(CT_mm, b + 1)
                nc.scalar.copy(CT[:, b], bank[4 + b % 4][:].rearrange("p (g n) -> p g n", g=HG)).then_inc(CT_odd, 1)
            for b in range(1, B, 2):
                act.wait_ge(U_mm, b + 1)
                nc.scalar.copy(U[:, b], bank[b % 4][:].rearrange("p (g d) -> p g d", g=HG)).then_inc(U_odd, 1)
            act.wait_ge(var_ready, 1)
            nc.scalar.activation(stat("sd"), stat("sd"), ACT.Sqrt).then_inc(std_ready, 1)
            for n in range(2):
                act.wait_ge(cs_mm, n + 1)
                nc.scalar.activation(gx[:, 4 * n:4 * n + 4, :], bank[2 + n][0:S, :].rearrange("p (b n) -> p b n", b=4),
                                     ACT.Gelu_apprx_tanh).then_inc(gx_ready, 1)
            act.wait_ge(var_ready, 2)
            nc.scalar.activation(stat("sd"), stat("sd"), ACT.Sqrt).then_inc(std_ready, 1)
            act.wait_ge(gate_shift, 1)
            nc.scalar.activation(stat("gp"), stat("gp"), ACT.Exp).then_inc(gate_exp, 1)
            act.wait_ge(expert_ready, 1)
            experts = [act.value_load(expert_u[0:1, j:j + 1], min_val=0, max_val=E - 1) for j in range(NB)]
            for j in range(NB):
                act.wait_ge(hn_mm, j + 1)
                if j >= 3:
                    act.wait_ge(down_mm, j - 2)
                for k in range(FK):
                    nc.scalar.activation(hT[:, j % 3, P * k:P * k + P], bank[2 + j % 2][:, P * k:P * k + P], ACT.Gelu,
                                         bias=b1T3[:, experts[j], k:k + 1]).then_inc(h_ready, 1)
            act.wait_ge(var_ready, 3)
            nc.scalar.activation(stat("sd"), stat("sd"), ACT.Sqrt).then_inc(std_ready, 1)

        @block.vector
        def _(dve):
            v = nc.vector
            count = [0]

            def step(ins):
                ins.then_inc(ve, 1)
                count[0] += 1

            def settle():
                dve.wait_ge(ve, count[0])

            for i in range(2):
                dve.wait_ge(xT_mm, i + 1)
                v.tensor_copy(xT[:, BANK * i:BANK * (i + 1)], bank[i][:]).then_inc(xT_ready, 1)
            dve.wait_ge(xT_ready, 2)
            v.tensor_reduce(xl[:], xT[:].rearrange("p (c l) -> p c l", l=L), AX_X, ALU.add).then_inc(xl_ready, 1)
            for p in range(0, PAIRS, 2):
                dve.wait_ge(qkl_mm, p + 1)
                v.tensor_copy(qkl[:, p], bank[(2 + p) % 8][:].rearrange("p (w c) -> p w c", w=2)).then_inc(qkl_even, 1)
            for i in range(2):
                g = slice(16 * i, 16 * i + 16)
                ps = bank[2 + i][:].rearrange("p (g m) -> p g m", g=16)
                dve.wait_ge(sim2_mm, i + 1)
                step(v.tensor_reduce(stat("mx2", 16 * i, 16), ps, AX_X, ALU.max))
                settle()
                v.tensor_tensor(A2[:, g], ps, stat("mx2", 16 * i, 16).unsqueeze(2).broadcast_to([P, 16, M]),
                                ALU.subtract).then_inc(sim2_shift, 1)
            for i in range(2):
                g = slice(16 * i, 16 * i + 16)
                dve.wait_ge(sim2_exp, i + 1)
                step(v.tensor_reduce(stat("rs2", 16 * i, 16), A2[:, g], AX_X, ALU.add))
                settle()
                step(v.reciprocal(stat("rs2", 16 * i, 16), stat("rs2", 16 * i, 16)))
                settle()
                v.tensor_tensor(A2[:, g], A2[:, g], stat("rs2", 16 * i, 16).unsqueeze(2).broadcast_to([P, 16, M]),
                                ALU.mult).then_inc(A2_ready, 1)
            dve.wait_ge(A2_ready, 2)
            v.transpose(A2T[:].rearrange("p g m -> p (g m)"), A2[:].rearrange("p g m -> p (g m)")).then_inc(A2T_ready, 1)
            step(v.tensor_reduce(stat("cs"), A2[:], AX_X, ALU.add))
            dve.wait_ge(A2T_ready, 1)
            step(v.tensor_reduce(stat("rows"), A2T[:], AX_X, ALU.add))
            settle()
            step(v.tensor_reduce(stat("peak", 0, 1), stat("cs"), AX_X, ALU.max))
            v.tensor_reduce(stat("peak", 1, 1), stat("rows"), AX_X, ALU.max).then_inc(peak_ready, 1)
            for h in range(1, H, 2):
                dve.wait_ge(GG_mm, h + 1)
                v.tensor_copy(GG[:, :, :, h, :].rearrange("p b w m -> p w b m"),
                bank[(2 + h) % 8][:].rearrange("p (w b m) -> p w b m", w=2, b=B)).then_inc(GG_odd, 1)
            dve.wait_ge(peak_mm, 1)
            step(v.tensor_reduce(stat("pk")[0:1, :], bank[6][0:1, 0:256].rearrange("p (w n) -> p w n", w=2),
                                 AX_X, ALU.max))
            settle()
            step(v.tensor_tensor(stat("prod")[0:1, :], stat("pk", 0, 1)[0:1, :], stat("pk", 1, 1)[0:1, :], ALU.mult))
            settle()
            v.reciprocal(stat("cinv")[0:1, :], stat("prod")[0:1, :]).then_inc(cinv_ready, 1)
            dve.wait_ge(c_mm, 1)
            v.tensor_copy(stat("c"), bank[6][:, 256:257]).then_inc(c_ready, 1)
            for s in range(B + 3):
                if s < B:
                    ps = bank[1 + s % 2][:].rearrange("p (h m) -> p h m", h=H)
                    dve.wait_ge(sim1_mm, s + 1)
                    step(v.tensor_reduce(stat("mx1", H * s, H), ps, AX_X, ALU.max))
                    dve.wait_ge(sim3_mm, s + 1)
                    step(v.tensor_reduce(stat("nm3", HG * s, HG),
                                         bank[5 + s % 2][:].rearrange("p (g n) -> p g n", g=HG), AX_X, ALU.max))
                    settle()
                    v.tensor_tensor(A1[:, s], ps, stat("mx1", H * s, H).unsqueeze(2).broadcast_to([P, H, M]),
                                    ALU.subtract).then_inc(sim1_shift, 1)
                    v.tensor_scalar(stat("nm3", HG * s, HG), stat("nm3", HG * s, HG), -DH ** -0.5 / L, None,
                                    ALU.mult).then_inc(max3_ready, 1)
                if 3 <= s:
                    b = s - 3
                    dve.wait_ge(E3T_mm, b + 1)
                    if b >= 2:
                        dve.wait_ge(YT_mm, b - 1)
                    v.tensor_copy(E3T[:, b % 2, :], bank[7][:]).then_inc(E3T_ready, 1)
                if 1 <= s < B + 1:
                    b = s - 1
                    dve.wait_ge(exp3_done, HG * (b + 1))
                    v.reciprocal(stat("r3", HG * b, HG), stat("s3", HG * b, HG)).then_inc(rsum3, 1)
                    dve.wait_ge(exp1_done, b + 1)
                    step(v.tensor_reduce(stat("rs1", H * b, H), A1[:, b], AX_X, ALU.add))
                    settle()
                    v.reciprocal(stat("rs1", H * b, H), stat("rs1", H * b, H)).then_inc(rsum1, 1)
            dve.wait_ge(Qd_zero, 1)
            dve.wait_ge(const_ready, 1 + E + 4)
            for k in range(steps):
                c = k % CH
                g = slice(GC * c, GC * c + GC)
                if k >= CH:
                    dve.wait_ge(V_ready, 5 * (k - CH) + 1)
                else:
                    dve.wait_ge(P0_ready, 5 * (c // 2 + 1))
                    dve.wait_ge(W0_ready, c // 2 + 1)
                step(v.scalar_tensor_tensor(out=GB[:, g], in0=V[:, g, 0, :], scalar=QB,
                                            in1=eye_a[:].unsqueeze(1).broadcast_to([P, GC, M]),
                                            op0=ALU.mult, op1=ALU.add))
                dve.wait_ge(PV_mm, k + 1)
                ps = bank[c % 2][:].rearrange("p (g w m) -> p g w m", g=GC, w=2)
                v.scalar_tensor_tensor(out=MM[:, g].rearrange("p g w m -> p (g w m)"),
                                       in0=V[:, g].rearrange("p g w m -> p (g w m)"), scalar=ROOT,
                                       in1=bank[c % 2][:], op0=ALU.mult, op1=ALU.subtract).then_inc(MQ_ready, 1)
                settle()
                if k >= 3:
                    dve.wait_ge(QM_mm, k - 2)
                for q in range(4):
                    v.tensor_tensor(Qd[quad(q), k % 3, :, quad(q)], GB[quad(q), g], ps[quad(q), :, 0, :], ALU.add
                                    ).then_inc(MQ_ready, 1)
            for p in range(0, PAIRS, 2):
                dve.wait_ge(C_mm, p + 1)
                v.tensor_copy(CC[:, :, 2 * p:2 * p + 2].rearrange("p b h m -> p h b m"),
                              bank[4 + p % 4][:].rearrange("p (h b m) -> p h b m", h=2, b=B)).then_inc(C_even, 1)
            for b in range(0, B, 2):
                dve.wait_ge(CT_mm, b + 1)
                v.tensor_copy(CT[:, b], bank[4 + b % 4][:].rearrange("p (g n) -> p g n", g=HG)).then_inc(CT_even, 1)
            for b in range(0, B, 2):
                dve.wait_ge(U_mm, b + 1)
                v.tensor_copy(U[:, b], bank[b % 4][:].rearrange("p (g d) -> p g d", g=HG)).then_inc(U_even, 1)

            def layer_norm(n, src, dst, ready):
                settle()
                for b in range(B):
                    step(v.bn_stats(stat("bn", 6 * b, 6), src[:, b, :]))
                settle()
                for b in range(B):
                    step(v.bn_aggr(stat("mv", 2 * b, 2), stat("bn", 6 * b, 6)))
                settle()
                v.tensor_scalar(stat("sd"), stat("mv").rearrange("p (b w) -> p b w", w=2)[:, :, 1], EPS, None,
                                ALU.add).then_inc(var_ready, 1)
                dve.wait_ge(std_ready, n + 1)
                step(v.reciprocal(stat("rstd"), stat("sd")))
                settle()
                for b in range(B):
                    v.tensor_scalar(dst[:, b, :], src[:, b, :], stat("mv", 2 * b, 1), stat("rstd", b, 1),
                                    ALU.subtract, ALU.mult).then_inc(ready, 1)

            dve.wait_ge(xb_ready, 1)
            for n in range(2):
                dve.wait_ge(attn_mm, n + 1)
                step(v.tensor_tensor(y[:, 4 * n:4 * n + 4, :], xb[:, 4 * n:4 * n + 4, :],
                                     bank[4 + n][:].rearrange("p (b d) -> p b d", b=4), ALU.add))
            layer_norm(0, y, x1, x1_ready)
            for n in range(2):
                dve.wait_ge(x1T_mm, n + 1)
                v.tensor_copy(xTn[:, BANK * n:BANK * n + BANK], bank[n][:]).then_inc(x1T_ready, 1)
            dve.wait_ge(x1_ready, B)
            for n in range(2):
                dve.wait_ge(xa_mm, n + 1)
                step(v.tensor_tensor(y[:, 4 * n:4 * n + 4, :], x1[:, 4 * n:4 * n + 4, :],
                                     bank[4 + n][:].rearrange("p (b d) -> p b d", b=4), ALU.add))
            layer_norm(1, y, x2, x2_ready)
            for n in range(2):
                dve.wait_ge(x2T_mm, n + 1)
                v.tensor_copy(xTn[:, BANK * n:BANK * n + BANK], bank[n][:]).then_inc(x2T_ready, 1)
            be = [P, B, E]
            gl = bank[2][:, 0:B * E].rearrange("p (b e) -> p b e", b=B)
            gp = stat("gp").rearrange("p (b e) -> p b e", b=B)
            gm = stat("gm").rearrange("p (b e) -> p b e", b=B)
            cw = stat("cw").rearrange("p (b e) -> p b e", b=B)
            dve.wait_ge(gate_mm, 1)
            step(v.tensor_reduce(stat("gmx"), gl, AX_X, ALU.max))
            settle()
            v.tensor_tensor(gp, gl, stat("gmx").unsqueeze(2).broadcast_to(be), ALU.subtract).then_inc(gate_shift, 1)
            dve.wait_ge(gate_exp, 1)
            step(v.tensor_reduce(stat("grs"), gp, AX_X, ALU.add))
            settle()
            step(v.reciprocal(stat("grs"), stat("grs")))
            settle()
            step(v.tensor_tensor(gp, gp, stat("grs").unsqueeze(2).broadcast_to(be), ALU.mult))
            settle()
            step(v.tensor_reduce(stat("gpm"), gp, AX_X, ALU.max))
            settle()
            step(v.tensor_tensor(gm, gp, stat("gpm").unsqueeze(2).broadcast_to(be), ALU.is_equal))
            settle()
            step(v.tensor_tensor(gm, gm, prio[:].unsqueeze(1).broadcast_to(be), ALU.mult))
            settle()
            step(v.tensor_reduce(stat("gsm"), gm, AX_X, ALU.max))
            settle()
            v.tensor_tensor(gm, gm, stat("gsm").unsqueeze(2).broadcast_to(be), ALU.is_equal).then_inc(sel_ready, 1)
            dve.wait_ge(sel_ready, 1)
            v.tensor_reduce(stat("nsel"), gm.rearrange("p b e -> p e b"), AX_X, ALU.add).then_inc(nsel_ready, 1)
            v.tensor_tensor(cw, gm, stat("gpm").unsqueeze(2).broadcast_to(be), ALU.mult).then_inc(cw_ready, 1)
            dve.wait_ge(route_const, 3 + 8 + NB + 1 + E)
            dve.wait_ge(rank_mm, 1)
            ee = [P, E, E]
            cmp3 = stat("cmp").rearrange("p (e k) -> p e k", e=E)
            step(v.tensor_tensor(cmp3, bank[2][:, B * E:B * E + E].unsqueeze(2).broadcast_to(ee),
                                 full_at[:].unsqueeze(1).broadcast_to(ee), ALU.is_gt))
            settle()
            step(v.tensor_reduce(stat("nb"), cmp3, AX_X, ALU.add))
            settle()
            step(v.tensor_tensor(cmp3, upto[:], stat("nb").unsqueeze(1).broadcast_to(ee), ALU.mult))
            settle()
            step(v.tensor_reduce(stat("cum"), cmp3, AX_X, ALU.add))
            settle()
            step(v.tensor_tensor(stat("start"), stat("cum"), stat("nb"), ALU.subtract))
            bcmp = stat("bcmp")[0:1, :].rearrange("p (j e) -> p j e", j=NB)
            step(v.tensor_tensor(bcmp, stat("cum")[0:1, :].unsqueeze(1).broadcast_to([1, NB, E]),
                                 block_no[:].unsqueeze(2).broadcast_to([1, NB, E]), ALU.is_le))
            settle()
            step(v.tensor_reduce(stat("bexp")[0:1, :], bcmp, AX_X, ALU.add))
            slots = stat("slots").rearrange("p (b e) -> p b e", b=B)
            step(v.scalar_tensor_tensor(out=slots, in0=stat("start").unsqueeze(1).broadcast_to(be), scalar=float(P),
                                        in1=bank[3][:, 0:B * E].rearrange("p (b e) -> p b e", b=B),
                                        op0=ALU.mult, op1=ALU.add))
            settle()
            v.tensor_scalar(expert_u[:], stat("bexp")[0:1, :], float(E - 1), None, ALU.min).then_inc(expert_ready, 1)
            step(v.tensor_tensor(slots, slots, gm, ALU.mult))
            settle()
            step(v.tensor_reduce(stat("slot"), slots, AX_X, ALU.add))
            settle()
            v.tensor_copy(slot_u[:], stat("slot")).then_inc(slot_ready, 1)
            for n in range(2):
                dve.wait_ge(cwT_mm, n + 1)
                v.tensor_copy(cwT[:, BANK * n:BANK * n + BANK], bank[6 + n][0:E, :]).then_inc(cwT_ready, 1)
            dve.wait_ge(x2_ready, B)
            dve.wait_ge(cw_ready, 1)
            for n in range(2):
                dve.wait_ge(b2_mm, n + 1)
                v.tensor_tensor(acc[:, 4 * n:4 * n + 4, :], x2[:, 4 * n:4 * n + 4, :],
                                bank[4 + n][:].rearrange("p (b d) -> p b d", b=4), ALU.add).then_inc(base_ready, 1)
            for n in range(4):
                w = 4 if n < 3 else NB - 12
                dve.wait_ge(xsT_mm, n + 1)
                v.tensor_copy(xsT[:, 4 * n:4 * n + w, :], bank[n][:, 0:P * w].rearrange("p (j t) -> p j t", j=w)
                              ).then_inc(xsT_ready, 1)
            for s in range(NB + 2):
                if s < NB:
                    dve.wait_ge(up_mm, s + 1)
                    if s >= 3:
                        dve.wait_ge(hn_mm, s - 2)
                    v.tensor_copy(hn[:, s % 3, :], bank[s % 2][:]).then_inc(hn_ready, 1)
                if s >= 2:
                    j = s - 2
                    dve.wait_ge(down_mm, j + 1)
                    v.tensor_copy(ys[:, j, :], bank[4 + j % 2][:, 0:D]).then_inc(ys_ready, 1)
            dve.wait_ge(base_ready, 2)
            for b in range(B):
                dve.wait_ge(yg_loaded[b], 16)
                v.scalar_tensor_tensor(out=acc[:, b, :], in0=yg[:, b, :], scalar=stat("gpm", b, 1), in1=acc[:, b, :],
                                       op0=ALU.mult, op1=ALU.add).then_inc(acc_ready, 1)
            dve.wait_ge(acc_ready, B)
            layer_norm(2, acc, fin, fin_ready)


INS = ["x", "ctx_1024", "L0_attn_w_qkv", "L0_attn_w_conv", "L0_attn_w_fc", "L0_attn_b_fc", "L0_ffn_gate_w",
       "L0_ffn_w1", "L0_ffn_b1", "L0_ffn_w2", "L0_ffn_b2"]


def kernel(**inputs):
    import numpy as np
    import concourse.bacc as bacc
    from concourse.bass_utils import run_bass_kernel_spmd

    nc = bacc.Bacc("TRN2", target_bir_lowering=False, num_devices=1)
    arrays, args = {}, []
    for name in INS:
        a = np.ascontiguousarray(inputs[name])
        arrays["in_" + name] = a
        args.append(nc.dram_tensor("in_" + name, a.shape, mybir.dt.from_np(a.dtype), kind="ExternalInput").ap())
    args.append(nc.dram_tensor("out_x", (B, N, D), F32, kind="ExternalOutput").ap())
    program(nc, *args)
    r = run_bass_kernel_spmd(nc, [arrays], core_ids=[0])
    return r.results[0]["out_x"]
```
